# Optimizing a Trainium2 kernel written in Bass

```python
import numpy as np
import jax
import jax.numpy as jnp

def _softmax(x, axis=-1):
    return jax.nn.softmax(x, axis=axis)

def _gelu(x):
    return jax.nn.gelu(x, approximate=True)

def _silu(x):
    return jax.nn.silu(x)

def _sigmoid(x):
    return jax.nn.sigmoid(x)

def _layernorm(x, axis=-1, eps=1e-05):
    m = jnp.mean(x, axis=axis, keepdims=True)
    v = jnp.var(x, axis=axis, keepdims=True)
    return (x - m) / jnp.sqrt(v + eps)

def _scatter_add(tgt, idx, src, axis=0):
    return tgt.at[idx].add(src)

def _segment_sum(src, seg, n):
    return jax.ops.segment_sum(src, seg, n)
kernel_name = 'mk_sandwich_d1_jaxref_r4_60825c'

def setup_inputs(seed: int=0):
    np.random.seed(seed)
    _w = jnp.asarray

    def _L0_attn_setup():
        import jax, jax.numpy as jnp
        import numpy as np
        H = 16
        KVH = 4
        D = 128
        HID = 512
        EPS = 1e-06
        GROUPS = H // KVH

        def elu_plus_one(x):
            return jax.nn.elu(x) + 1.0

        def _repeat_kv(x, b, s):
            x = x.reshape(b, s, KVH, 1, D)
            x = jnp.broadcast_to(x, (b, s, KVH, GROUPS, D))
            return x.reshape(b, s, H * D)

        def _split_heads(x, b, s, nh):
            return x.reshape(b, s, nh, D).transpose(0, 2, 1, 3)
        key = jax.random.key(seed)
        ks = jax.random.split(key, 8)
        s = 0.02
        return {'hidden_states': jax.random.normal(ks[0], (2, 1024, HID), jnp.float32), 'Wq': jax.random.normal(ks[1], (H * D, HID), jnp.float32) * s, 'bq': jnp.zeros((H * D,), jnp.float32), 'Wk': jax.random.normal(ks[2], (KVH * D, HID), jnp.float32) * s, 'bk': jnp.zeros((KVH * D,), jnp.float32), 'Wv': jax.random.normal(ks[3], (KVH * D, HID), jnp.float32) * s, 'bv': jnp.zeros((KVH * D,), jnp.float32), 'Wo': jax.random.normal(ks[4], (HID, H * D), jnp.float32) * s}
    _L0_attn_in = _L0_attn_setup()

    def _L0_ffn_setup():
        import jax, jax.numpy as jnp
        import numpy as np
        E = 32
        G = 8
        TKG = 4
        K = 4
        D = 512
        H = 256
        HS = 1024
        SCALE = 2.5
        CAP = 256

        def relu2(x):
            r = jnp.maximum(x, 0.0)
            return r * r

        def route_tokens(scores, bias_corr):
            T = scores.shape[0]
            scores_c = scores + bias_corr
            group_scores = jax.lax.top_k(scores_c.reshape(T, G, E // G), 2)[0].sum(-1)
            _, group_idx = jax.lax.top_k(group_scores, TKG)
            group_mask = jnp.zeros((T, G), scores.dtype).at[jnp.arange(T)[:, None], group_idx].set(1.0)
            score_mask = jnp.repeat(group_mask, E // G, axis=1)
            masked = jnp.where(score_mask > 0, scores_c, 0.0)
            _, topk_idx = jax.lax.top_k(masked, K)
            topk_w = jnp.take_along_axis(scores, topk_idx, axis=1)
            topk_w = topk_w / (topk_w.sum(-1, keepdims=True) + 1e-20)
            return (topk_idx, topk_w * SCALE)
        key = jax.random.key(seed)
        ks = jax.random.split(key, 6)
        B, S = (2, 512)
        return dict(hidden_states=jax.random.normal(ks[0], (B, S, D), jnp.float32), gate_w=jax.random.normal(ks[1], (E, D), jnp.float32) * 0.02, bias_corr=jnp.zeros((E,), jnp.float32), up_w=jax.random.normal(ks[2], (E, H, D), jnp.float32) * 0.02, down_w=jax.random.normal(ks[3], (E, D, H), jnp.float32) * 0.02, shared_up_w=jax.random.normal(ks[4], (HS, D), jnp.float32) * 0.02, shared_down_w=jax.random.normal(ks[5], (D, HS), jnp.float32) * 0.02)
    _L0_ffn_in = _L0_ffn_setup()
    _d = {'L0_attn_hidden_states': _L0_attn_in['hidden_states'], 'L0_attn_Wq': _L0_attn_in['Wq'], 'L0_attn_bq': _L0_attn_in['bq'], 'L0_attn_Wk': _L0_attn_in['Wk'], 'L0_attn_bk': _L0_attn_in['bk'], 'L0_attn_Wv': _L0_attn_in['Wv'], 'L0_attn_bv': _L0_attn_in['bv'], 'L0_attn_Wo': _L0_attn_in['Wo'], 'L0_ffn_gate_w': _L0_ffn_in['gate_w'], 'L0_ffn_bias_corr': _L0_ffn_in['bias_corr'], 'L0_ffn_up_w': _L0_ffn_in['up_w'], 'L0_ffn_down_w': _L0_ffn_in['down_w'], 'L0_ffn_shared_up_w': _L0_ffn_in['shared_up_w'], 'L0_ffn_shared_down_w': _L0_ffn_in['shared_down_w']}
    _x0 = _d['L0_attn_hidden_states']
    _d['L0_attn_hidden_states'] = jax.random.normal(jax.random.fold_in(jax.random.key(seed), 1), (4, 1024, 512), dtype=_x0.dtype)
    del _x0
    return _d

def reference(L0_attn_hidden_states, L0_attn_Wq, L0_attn_bq, L0_attn_Wk, L0_attn_bk, L0_attn_Wv, L0_attn_bv, L0_attn_Wo, L0_ffn_gate_w, L0_ffn_bias_corr, L0_ffn_up_w, L0_ffn_down_w, L0_ffn_shared_up_w, L0_ffn_shared_down_w):

    def _L0_attn_ref(hidden_states, Wq, bq, Wk, bk, Wv, bv, Wo):
        import jax, jax.numpy as jnp
        import numpy as np
        H = 16
        KVH = 4
        D = 128
        HID = 512
        EPS = 1e-06
        GROUPS = H // KVH

        def elu_plus_one(x):
            return jax.nn.elu(x) + 1.0

        def _repeat_kv(x, b, s):
            x = x.reshape(b, s, KVH, 1, D)
            x = jnp.broadcast_to(x, (b, s, KVH, GROUPS, D))
            return x.reshape(b, s, H * D)

        def _split_heads(x, b, s, nh):
            return x.reshape(b, s, nh, D).transpose(0, 2, 1, 3)
        b, s, _ = hidden_states.shape
        q = hidden_states @ Wq.T + bq
        k = hidden_states @ Wk.T + bk
        v = hidden_states @ Wv.T + bv
        k = _repeat_kv(k, b, s)
        v = _repeat_kv(v, b, s)
        q = _split_heads(q, b, s, H)
        k = _split_heads(k, b, s, H)
        v = _split_heads(v, b, s, H)
        sq = elu_plus_one(q)
        sk = elu_plus_one(k)
        kv = jnp.einsum('bhsd,bhse->bhde', sk, v)
        qkv = jnp.einsum('bhsd,bhde->bhse', sq, kv)
        k_sum = sk.sum(axis=2)
        norm = jnp.einsum('bhsd,bhd->bhs', sq, k_sum)
        attn = qkv / (norm[..., None] + EPS)
        attn = attn.transpose(0, 2, 1, 3).reshape(b, s, H * D)
        return attn @ Wo.T

    def _L0_ffn_ref(hidden_states, gate_w, bias_corr, up_w, down_w, shared_up_w, shared_down_w):
        import jax, jax.numpy as jnp
        import numpy as np
        E = 32
        G = 8
        TKG = 4
        K = 4
        D = 512
        H = 256
        HS = 1024
        SCALE = 2.5
        CAP = 256

        def relu2(x):
            r = jnp.maximum(x, 0.0)
            return r * r

        def route_tokens(scores, bias_corr):
            T = scores.shape[0]
            scores_c = scores + bias_corr
            group_scores = jax.lax.top_k(scores_c.reshape(T, G, E // G), 2)[0].sum(-1)
            _, group_idx = jax.lax.top_k(group_scores, TKG)
            group_mask = jnp.zeros((T, G), scores.dtype).at[jnp.arange(T)[:, None], group_idx].set(1.0)
            score_mask = jnp.repeat(group_mask, E // G, axis=1)
            masked = jnp.where(score_mask > 0, scores_c, 0.0)
            _, topk_idx = jax.lax.top_k(masked, K)
            topk_w = jnp.take_along_axis(scores, topk_idx, axis=1)
            topk_w = topk_w / (topk_w.sum(-1, keepdims=True) + 1e-20)
            return (topk_idx, topk_w * SCALE)
        B, S, _ = hidden_states.shape
        T = B * S
        flat = hidden_states.reshape(T, D)
        logits = flat @ gate_w.T
        scores = jax.nn.sigmoid(logits)
        topk_idx, topk_w = route_tokens(scores, bias_corr)
        e_flat = topk_idx.reshape(-1)
        oh = jax.nn.one_hot(e_flat, E, dtype=jnp.int32)
        pos = jnp.take_along_axis(jnp.cumsum(oh, axis=0) - 1, e_flat[:, None], axis=1)[:, 0]
        tok = jnp.repeat(jnp.arange(T), K)
        valid = pos < CAP
        xe = jnp.zeros((E, CAP, D), flat.dtype).at[e_flat, pos].set(flat[tok], mode='drop')
        h = relu2(jnp.einsum('ecd,ehd->ech', xe, up_w))
        ye = jnp.einsum('ech,edh->ecd', h, down_w)
        gathered = ye[e_flat, jnp.minimum(pos, CAP - 1)]
        gathered = jnp.where(valid[:, None], gathered, 0.0) * topk_w.reshape(-1)[:, None]
        routed = gathered.reshape(T, K, D).sum(axis=1).reshape(B, S, D)
        shared = relu2(hidden_states @ shared_up_w.T) @ shared_down_w.T
        return routed + shared
    x = L0_attn_hidden_states
    x = x + _layernorm(_L0_attn_ref(_layernorm(x, axis=-1), L0_attn_Wq, L0_attn_bq, L0_attn_Wk, L0_attn_bk, L0_attn_Wv, L0_attn_bv, L0_attn_Wo), axis=-1)
    x = x + _layernorm(_L0_ffn_ref(_layernorm(x, axis=-1), L0_ffn_gate_w, L0_ffn_bias_corr, L0_ffn_up_w, L0_ffn_down_w, L0_ffn_shared_up_w, L0_ffn_shared_down_w), axis=-1)
    return x

_drawn_inputs = setup_inputs


def setup_inputs(seed=0):
    import zlib

    import numpy as np

    out = dict(_drawn_inputs(seed))
    spreads = {'L0_attn_bq': (0.0, 0.8),
     'L0_attn_bk': (0.0, 0.8),
     'L0_attn_bv': (0.0, 0.1),
     'L0_ffn_bias_corr': (0.0, 0.1)}
    factors = {'L0_attn_Wq': 5.83, 'L0_attn_Wk': 2.946}
    for name, (base, spread) in spreads.items():
        noise = np.random.default_rng([zlib.crc32(name.encode()), seed]).standard_normal(out[name].shape)
        drawn = base * np.exp(spread * noise) if base else spread * noise
        out[name] = jnp.asarray(drawn.astype(out[name].dtype))
    for name, factor in factors.items():
        out[name] = (out[name] * factor).astype(out[name].dtype)
    return out
```

```python
from contextlib import ExitStack

import concourse.bass as bass
from concourse import mybir

F32 = mybir.dt.float32
F32R = mybir.dt.float32r
BF16 = mybir.dt.bfloat16
U32 = mybir.dt.uint32
ALU = mybir.AluOpType
ACT = mybir.ActivationFunctionType
AX = mybir.AxisListType

P = 128
B, S, C = 4, 1024, 512
T = B * S
NT = T // P
KC = C // P
CH = 512
NCH = T // CH
TPC = CH // P
TPB = S // P
H, G, D = 16, 4, 128
HPG = H // G
HD2 = G * D
NE, NG, TOPG, TOPK = 32, 8, 4, 4
EPG = NE // NG
CAP = 256
NSLOT = NE * CAP
FE, FS = 256, 1024
LN_EPS, NORM_EPS, SCALE = 1e-5, 1e-6, 2.5
SKIP = float(1 << 20)

assert G == TPC and NT == NCH * G


def ds(i, k=1):
    return bass.ds(i, k)


def known(v):
    return isinstance(v, int)


def back(n, j, lag):
    return (n, j - lag) if j >= lag else (n - 1, j - lag + HPG)


def due(value):
    return max(value, 0) if known(value) else value


def three(pe, out, lhs, rhs, first=True, last=True):
    pe.matmul(out, lhs[0], rhs[0], start=first, stop=False, skip_group_check=True)
    pe.matmul(out, lhs[0], rhs[1], start=False, stop=False, skip_group_check=True)
    return pe.matmul(out, lhs[1], rhs[0], start=False, stop=last, skip_group_check=True)


def flat(ap):
    n = len(ap.shape)
    if n == 3:
        return ap.rearrange("p a n -> p (a n)")
    return ap.rearrange("p a c n -> p (a c) n")


SCATTERS = {(1, 2): (0, 3), (1, 3): (3, 7), (2, 0): (7, 10), (2, 1): (10, 13), (2, 2): (13, 16)}
ROUTE = 49


def phase_attention(nc, d, x1, x2, slots, kept):
    slot_all, weight_all = kept
    with ExitStack() as ctx:
        def sb(name, shape, dt=F32):
            return ctx.enter_context(nc.sbuf_tensor("a_" + name, shape, dt))

        def sem(name):
            return ctx.enter_context(nc.semaphore("a_" + name))

        ident = sb("ident", [P, P])
        ones, ones_r = sb("ones", [P, P]), sb("ones_r", [P, P], F32R)
        keep = sb("keep", [P, TPB])
        power, zeros = sb("power", [P, TPC]), sb("zeros", [P, C])
        wk_h, wk_l = sb("wk_h", [P, KC, HD2], F32R), sb("wk_l", [P, KC, HD2], F32R)
        wv_h, wv_l = sb("wv_h", [P, KC, HD2], F32R), sb("wv_l", [P, KC, HD2], F32R)
        bq = sb("bq", [P, H])
        bkv = sb("bkv", [2, 2, HD2], F32R)
        xT_h, xT_l = sb("xT_h", [P, 3, KC, CH], F32R), sb("xT_l", [P, 3, KC, CH], F32R)
        kv, ksum = sb("kv", [P, 2, HD2]), sb("ksum", [P, 2, G])
        x_in, xn = sb("x_in", [P, C]), sb("xn", [P, C])
        stats, mv, rstd = sb("stats", [P, 6]), sb("mv", [P, 2]), sb("rstd", [P, 1])
        xt_h, xt_l = sb("xt_h", [P, KC, P], F32R), sb("xt_l", [P, KC, P], F32R)
        k_exp, sk = sb("k_exp", [P, HD2]), sb("sk", [P, HD2])
        sk_h, sk_l = sb("sk_h", [P, HD2], F32R), sb("sk_l", [P, HD2], F32R)
        v_h, v_l = sb("v_h", [P, HD2], F32R), sb("v_l", [P, HD2], F32R)
        wq_raw, wo_raw = sb("wq_raw", [P, 2, KC, P]), sb("wo_raw", [P, 2, C])
        wq_h, wq_l = sb("wq_h", [P, 2, KC, P], F32R), sb("wq_l", [P, 2, KC, P], F32R)
        wo_h, wo_l = sb("wo_h", [P, 2, C], F32R), sb("wo_l", [P, 2, C], F32R)
        q_both = sb("q_both", [P, 2, CH])
        q_exp, q_pos = q_both[:, 0, :], q_both[:, 1, :]
        sq, sqn = sb("sq", [P, 2, CH]), sb("sqn", [P, CH])
        sqn_h, sqn_l = sb("sqn_h", [P, CH], F32R), sb("sqn_l", [P, CH], F32R)
        rn = sb("rn", [P, TPC])
        kv_h, kv_l = sb("kv_h", [P, D], F32R), sb("kv_l", [P, D], F32R)
        o_h, o_l = sb("o_h", [P, 2, CH], F32R), sb("o_l", [P, 2, CH], F32R)
        acc = sb("acc", [P, 2, TPC, C])
        x_res, x_norm = sb("x_res", [P, 2, C]), sb("x_norm", [P, TPC, C])
        xt_norm = sb("xt_norm", [P, TPC, KC, P])
        stats1, mv1, rstd1 = sb("stats1", [P, TPC, 6]), sb("mv1", [P, TPC, 2]), sb("rstd1", [P, TPC])
        stats2, mv2, rstd2 = sb("stats2", [P, TPC, 6]), sb("mv2", [P, TPC, 2]), sb("rstd2", [P, TPC])
        before_me, bias = sb("before_me", [P, P]), sb("bias", [P, TPC, NE])
        iota = sb("iota", [P, TPC * TOPK, NE])
        iota_g = sb("iota_g", [P, TPC * NG, TOPG])
        gate = sb("gate", [P, KC, NE])
        ex, score, corr, masked = (sb(n, [P, TPC, NE]) for n in ("ex", "score", "corr", "masked"))
        hi2, lo2 = sb("hi2", [P, TPC * NG, 2]), sb("lo2", [P, TPC * NG, 2])
        top, second, third, gsum, gmask = (sb(n, [P, TPC * NG]) for n in ("top", "second", "third", "gsum", "gmask"))
        g8, gi, g_hot = sb("g8", [P, TPC, 8]), sb("gi", [P, TPC, 8], U32), sb("g_hot", [P, TPC, NG, TOPG])
        e8, ei = sb("e8", [P, TPC, 8]), sb("ei", [P, TPC, 8], U32)
        hot = sb("hot", [P, TPC, TOPK, NE])
        hot_part = xt_norm[:, 0, :, :].rearrange("p t (k e) -> p t k e", k=TOPK)
        chosen, earlier = sb("chosen", [P, TPC, NE]), sb("earlier", [P, TPC, NE])
        weight, place, over, slot_f, fits = (sb(n, [P, TPC, TOPK]) for n in ("weight", "place", "over", "slot_f", "fits"))
        wsum, winv = sb("wsum", [P, TPC]), sb("winv", [P, TPC])
        slot_of = sb("slot_of", [P, TPC, TOPK], U32)
        bkv_raw, bkv_low, bkv_high = sq[0:2, :, :], q_both[0:2, :, :], o_h[0:2, :, :]

        def bank(name):
            return ctx.enter_context(nc.psum_tensor("a_" + name, [P, CH], F32))

        out_ps = [bank(f"out_ps{t}") for t in range(TPC)]
        q_ps, n_ps, o_ps, m_ps = bank("q_ps"), bank("n_ps"), bank("o_ps"), bank("m_ps")
        BESIDE, ALONE = (m_ps, m_ps, m_ps, m_ps), (n_ps, q_ps, o_ps, out_ps[3])

        def blocks(ps):
            return ps[:, :].rearrange("p (c s) -> p c s", c=KC)
        by_expert = m_ps[:, 0:TPC * NE].rearrange("p (t e) -> p t e", t=TPC)

        in_const, in_x = sem("in_const"), sem("in_x")
        in_wq, in_wo, in_res = ([sem(f"in_{n}{r}") for r in range(2)] for n in ("wq", "wo", "res"))
        st_zero = sem("st_zero")
        acc_free = sem("acc_free")
        a_set, p_set, d_set = sem("a_set"), sem("p_set"), sem("d_set")
        d_stat, d_xn = sem("d_stat"), sem("d_xn")
        p_rstd = sem("p_rstd")
        t_xt, a_xt, d_xt, a_xT = sem("t_xt"), sem("a_xt"), sem("d_xt"), sem("a_xT")
        t_k, a_k, d_sk, a_skh, p_skl = sem("t_k"), sem("a_k"), sem("d_sk"), sem("a_skh"), sem("p_skl")
        t_v, a_vh, d_vl = sem("t_v"), sem("a_vh"), sem("d_vl")
        t_ks, d_ks, t_kv, d_kv = sem("t_ks"), sem("d_ks"), sem("t_kv"), sem("d_kv")
        a_wq, p_wq, a_wo, p_wo = sem("a_wq"), sem("p_wq"), sem("a_wo"), sem("p_wo")
        t_q, a_q, d_sq = sem("t_q"), sem("a_q"), sem("d_sq")
        t_n, d_rn, t_b = sem("t_n"), sem("d_rn"), sem("t_b")
        d_sqn, a_sqh, p_sql = sem("d_sqn"), sem("a_sqh"), sem("p_sql")
        d_kvg = sem("d_kvg")
        t_o, a_oh, d_ol = sem("t_o"), sem("a_oh"), sem("d_ol")
        t_w, d_acc = sem("t_w"), sem("d_acc")

        st_norm, st_slots = sem("st_norm"), sem("st_slots")
        d_stat1, d_stat2 = sem("d_stat1"), sem("d_stat2")
        p_rstd1, p_rstd2 = sem("p_rstd1"), sem("p_rstd2")
        d_y, d_mid, d_norm = sem("d_y"), sem("d_mid"), sem("d_norm")
        t_xn, a_xn = sem("t_xn"), sem("a_xn")
        t_logit, a_ex, t_place, d_route = sem("t_logit"), sem("a_ex"), sem("t_place"), sem("d_route")
        STAT = 2 * TPC + 1
        CHOSEN, PRIOR, PLACED, SLOTS = 31, 34, 37, 41
        CONST = 16 * 13

        block = ctx.enter_context(nc.Block())

        def walk(eng, prep, attn):
            prep(0, True)
            with eng.Fori(1, TPB - 1) as m:
                prep(m, True)
            prep(TPB - 1, False)

            def chunk(c, tiles):
                for g in range(G):
                    attn(c * G + g, c, g, c * G + g + TPB if tiles else None)
            for c in range(3):
                chunk(c, True)
            with eng.Fori(3, NCH - 2) as c:
                chunk(c, True)
            with eng.Fori(NCH - 2, NCH) as c:
                chunk(c, False)
            chunk(NCH, False)
            chunk(NCH + 1, False)

        def live(k):
            return not known(k) or 0 <= k < NT * HPG

        def chunk_due(c, lag):
            return c - lag if not known(c) or 0 <= c - lag < NCH else None

        def turned_at(c, g):
            return (slice(None), ds(c % 3), slice(None), slice(g * P, (g + 1) * P))

        @block.sync
        def _(sp):
            sp.dma_start(ident[:, :], d["ident"]).then_inc(in_const, 16)
            sp.dma_start(ones[:, :], d["ones"]).then_inc(in_const, 16)
            sp.dma_start(keep[:, :], d["keep"]).then_inc(in_const, 16)
            sp.dma_start(bq[:, :], d["bq"]).then_inc(in_const, 16)
            for w, name in enumerate(("bk", "bv")):
                for row in range(2):
                    sp.dma_start(bkv_raw[row:row + 1, w, :], d[name]).then_inc(in_const, 16)

            def load_x(m):
                sp.dma_start(x_in[:, :], d["x"][ds(m), :, :].rearrange("a p c -> (a p) c")).then_inc(in_x, 16)

            def load_wq(k):
                sp.dma_start(wq_raw[:, k % 2, :, :].rearrange("p c d -> p (c d)"),
                             d["wq"][k % H, :, :]).then_inc(in_wq[k % 2], 16)

            def load_wo(k):
                sp.dma_start(wo_raw[:, k % 2, :], d["wo"][k % H, :, :]).then_inc(in_wo[k % 2], 16)

            for dst, name in ((before_me[:, :], "before_me"), (bias[:, :, :], "bias_corr"), (iota[:, :, :], "iota"),
                              (iota_g[:, :, :], "iota_g"), (gate[:, :, :], "gate")):
                sp.dma_start(dst, d[name]).then_inc(in_const, 16)
            sp.wait_ge(p_set, 2)
            load_x(0)
            sp.dma_start(acc[:, 0, :, :], d["wk"]).then_inc(acc_free, 16)
            sp.dma_start(acc[:, 1, :, :], d["wv"]).then_inc(acc_free, 16)
            load_wq(0)
            load_wq(1)

            def prep(m, ahead):
                sp.wait_ge(d_xn, m + 1)
                load_x(m + 1)

            def load_res(e, t):
                sp.wait_ge(d_mid, due(TPC * e + t - 1))
                sp.dma_start(x_res[:, t % 2, :], d["x"][ds(e * TPC + t), :, :].rearrange(
                    "a p c -> (a p) c")).then_inc(in_res[t % 2], 16)

            def rows(store, e):
                return store[ds(e * TPC, TPC), :, :].rearrange("t p c -> p t c")

            def beside(c, g, j):
                e = chunk_due(c, 1)
                if e is None:
                    return
                if (g, j) == (1, 0):
                    load_res(e, 0)
                    load_res(e, 1)
                if (g, j) == (2, 0):
                    load_res(e, 2)
                    load_res(e, 3)
                if (g, j) == (2, 2):
                    sp.wait_ge(d_mid, TPC * (e + 1))
                    sp.dma_start(rows(x1, e), acc[:, ds(e % 2), :, :].rearrange(
                        "p a t c -> p (a t) c")).then_inc(acc_free, 16)
                if (g, j) == (3, 1):
                    sp.wait_ge(d_norm, TPC * (e + 1))
                    sp.nop(nofuse=True)
                    sp.wait_ge(st_norm, 16 * e)
                    sp.nop(nofuse=True)
                    sp.dma_start(rows(x2, e), x_norm[:, :, :]).then_inc(st_norm, 16)

            def attn(n, c, g, m):
                for j in range(HPG):
                    k = n * HPG + j
                    if live(k):
                        if m is not None and j == 1:
                            sp.wait_ge(d_xn, m + 1)
                            load_x((m + 1) % NT)
                        sp.wait_ge(p_wq, k + 1)
                        load_wq(g * HPG + j + 2)
                        sp.wait_ge(p_wo, due(k - 1))
                        load_wo(g * HPG + j)
                    beside(c, g, j)
                if known(n) and n < 2 * G:
                    part = NSLOT // (2 * G)
                    sp.dma_start(slots[n * part:(n + 1) * part, :].rearrange("(p r) c -> p r c", p=P),
                                 zeros[:, :].rearrange("p (a c) -> p a c", a=1).to_broadcast(
                                     [P, part // P, C])).then_inc(st_zero, 16)

            walk(sp, prep, attn)
            sp.wait_ge(acc_free, 16 * (NCH + 2))
            sp.wait_ge(st_norm, 16 * NCH)
            sp.wait_ge(st_zero, 16 * 2 * G)
            sp.wait_ge(in_x, 16 * (NT + 1))
            for r in range(2):
                sp.wait_ge(in_wq[r], 16 * (NT * HPG // 2 + 1))

        @block.gpsimd
        def _(pool):
            pool.memset(power[:, :], -0.5).then_inc(p_set, 1)
            pool.memset(zeros[:, :], 0.0).then_inc(p_set, 1)
            pool.wait_ge(p_set, 2)

            def reciprocal_deviation(m):
                pool.wait_ge(d_stat, 3 * m + 3)
                pool.wait_ge(d_xn, m)
                pool.tensor_tensor(rstd[:, :], mv[:, 1:2], power[:, 0:1], ALU.pow).then_inc(p_rstd, 1)

            def keys_low(m):
                pool.wait_ge(a_skh, m + 1)
                pool.wait_ge(t_kv, m)
                pool.tensor_tensor(sk_l[:, :], sk[:, :], sk_h[:, :].bitcast(F32), ALU.subtract).then_inc(p_skl, 1)

            def wq_low(n, j):
                k = n * HPG + j
                pool.wait_ge(a_wq, k + 1)
                pool.wait_ge(t_q, due(k - 1))
                pool.tensor_tensor(wq_l[:, j % 2, :, :], wq_raw[:, j % 2, :, :],
                                   wq_h[:, j % 2, :, :].bitcast(F32), ALU.subtract).then_inc(p_wq, 1)

            def wo_low(n, j):
                k = n * HPG + j
                pool.wait_ge(a_wo, k + 1)
                pool.wait_ge(t_w, due(4 * (k - 1)))
                pool.tensor_tensor(wo_l[:, j % 2, :], wo_raw[:, j % 2, :], wo_h[:, j % 2, :].bitcast(F32),
                                   ALU.subtract).then_inc(p_wo, 1)

            def sqn_low(n, j):
                k = n * HPG + j
                pool.wait_ge(a_sqh, k + 1)
                pool.wait_ge(t_o, k)
                pool.tensor_tensor(sqn_l[:, :], sqn[:, :], sqn_h[:, :].bitcast(F32),
                                   ALU.subtract).then_inc(p_sql, 1)

            def scatter(e, first, last):
                pool.wait_ge(d_route, ROUTE * e + SLOTS)
                pool.nop(nofuse=True)
                for i in range(first, last):
                    t, k = i // TOPK, i % TOPK
                    pool.indirect_dma_start(slots, bass.IndirectOffsetOnAxis(ap=slot_of[:, t, k:k + 1], axis=0),
                                            x_norm[:, t, :], None, bounds_check=NSLOT - 1,
                                            oob_is_err=False).then_inc(st_slots, 16)

            def beside(c, g, j):
                e = chunk_due(c, 1)
                if e is not None and (g, j) == (1, 2):
                    pool.wait_ge(d_stat1, STAT * (e + 1))
                    pool.wait_ge(d_y, TPC * e)
                    pool.tensor_tensor(rstd1[:, :], mv1[:, :, 1], power[:, :], ALU.pow).then_inc(p_rstd1, 1)
                if e is not None and (g, j) == (2, 3):
                    pool.wait_ge(d_stat2, STAT * (e + 1))
                    pool.wait_ge(d_norm, TPC * e)
                    pool.tensor_tensor(rstd2[:, :], mv2[:, :, 1], power[:, :], ALU.pow).then_inc(p_rstd2, 1)
                e = chunk_due(c, 2)
                if e is not None and (g, j) in SCATTERS:
                    if known(e) and e == 0 and (g, j) == (1, 2):
                        pool.wait_ge(st_zero, 16 * 2 * G)
                    scatter(e, *SCATTERS[g, j])

            def prep(m, ahead):
                if known(m) and m == 0:
                    reciprocal_deviation(0)
                if ahead:
                    reciprocal_deviation(m + 1)
                keys_low(m)
                if known(m) and m == 0:
                    wq_low(0, 0)

            def slot(n, j, c, g, m):
                k = n * HPG + j
                if live(k - 2):
                    sqn_low(*back(n, j, 2))
                if live(k + 1):
                    wq_low(*((n, j + 1) if j < HPG - 1 else (n + 1, 0)))
                if m is not None and j == 0:
                    reciprocal_deviation(m)
                if live(k - 2):
                    wo_low(*back(n, j, 2))
                if m is not None and j == 2:
                    keys_low(m)
                beside(c, g, j)

            def attn(n, c, g, m):
                for j in range(HPG):
                    slot(n, j, c, g, m)

            walk(pool, prep, attn)
            pool.wait_ge(st_slots, 16 * TOPK * NT)

        @block.scalar
        def _(act):
            def turned(m, ps=BESIDE):
                act.wait_ge(t_xt, m + 1)
                act.wait_ge(t_v, m)
                act.wait_ge(a_xT, 2 * m)
                act.activation(xt_h[:, :, :], blocks(ps[0]), ACT.Copy).then_inc(a_xt, 1)

            def keep_turned(c, g, m):
                act.wait_ge(a_xt, m + 1)
                act.activation(flat(xT_h[turned_at(c, g)]), xt_h[:, :, :], ACT.Copy).then_inc(a_xT, 1)
                act.wait_ge(d_xt, m + 1)
                act.activation(flat(xT_l[turned_at(c, g)]), xt_l[:, :, :], ACT.Copy).then_inc(a_xT, 1)

            def keys(m, ps=BESIDE):
                act.wait_ge(t_k, m + 1)
                act.wait_ge(p_skl, m)
                act.activation(k_exp[:, :], ps[1][:, :], ACT.Exp).then_inc(a_k, 1)
                act.activation(sk[:, :], ps[1][:, :], ACT.Relu).then_inc(a_k, 1)

            def keys_high(m):
                act.wait_ge(d_sk, m + 1)
                act.wait_ge(t_kv, m)
                act.activation(sk_h[:, :], sk[:, :], ACT.Copy).then_inc(a_skh, 1)

            def values(m, ps=BESIDE):
                act.wait_ge(t_v, m + 1)
                act.wait_ge(t_kv, m)
                act.activation(v_h[:, :], ps[2][:, :], ACT.Copy).then_inc(a_vh, 1)

            def wq_high(n, j):
                k = n * HPG + j
                act.wait_ge(in_wq[j % 2], 16 * (2 * n + j // 2 + 1))
                act.wait_ge(t_q, due(k - 1))
                act.wait_ge(p_wq, due(k - 1))
                act.activation(wq_h[:, j % 2, :, :], wq_raw[:, j % 2, :, :], ACT.Copy).then_inc(a_wq, 1)

            def wo_high(n, j):
                k = n * HPG + j
                act.wait_ge(in_wo[j % 2], 16 * (2 * n + j // 2 + 1))
                act.wait_ge(t_w, due(4 * (k - 1)))
                act.activation(wo_h[:, j % 2, :], wo_raw[:, j % 2, :], ACT.Copy).then_inc(a_wo, 1)

            def queries(n, j, g):
                k = n * HPG + j
                act.wait_ge(t_q, k + 1)
                act.wait_ge(d_sq, k)
                bias = bq[:, ds(g * HPG + j)]
                act.activation(q_exp, q_ps[:, :], ACT.Exp, bias=bias).then_inc(a_q, 1)
                act.activation(q_pos, q_ps[:, :], ACT.Relu, bias=bias).then_inc(a_q, 1)

            def sqn_high(n, j):
                k = n * HPG + j
                act.wait_ge(d_sqn, k + 1)
                act.wait_ge(t_o, k)
                act.activation(sqn_h[:, :], sqn[:, :], ACT.Copy).then_inc(a_sqh, 1)

            def o_high(n, j):
                k = n * HPG + j
                act.wait_ge(t_o, k + 1)
                act.wait_ge(t_w, due(4 * (k - 1)))
                act.activation(o_h[:, j % 2, :], o_ps[:, :], ACT.Copy).then_inc(a_oh, 1)

            def turned_alone(m):
                turned(m, ALONE)
                at = (slice(None), ds(m // TPC), slice(None), ds((m % TPC) * P, P))
                act.wait_ge(a_xt, m + 1)
                act.activation(flat(xT_h[at]), xt_h[:, :, :], ACT.Copy).then_inc(a_xT, 1)
                act.wait_ge(d_xt, m + 1)
                act.activation(flat(xT_l[at]), xt_l[:, :, :], ACT.Copy).then_inc(a_xT, 1)

            def prep(m, ahead):
                if known(m) and m == 0:
                    act.wait_ge(acc_free, 32)
                    act.activation(wk_h[:, :, :], acc[:, 0, :, :], ACT.Copy).then_inc(a_set, 1)
                    act.wait_ge(in_const, CONST)
                    turned_alone(0)
                    act.activation(wv_h[:, :, :], acc[:, 1, :, :], ACT.Copy).then_inc(a_set, 1)
                keys(m, ALONE)
                keys_high(m)
                values(m, ALONE)
                if ahead:
                    turned_alone(m + 1)
                if known(m) and m == 0:
                    wq_high(0, 0)

            def beside_norm(c):
                e = chunk_due(c, 1)
                if e is None:
                    return
                act.wait_ge(t_logit, e)
                act.wait_ge(d_route, due(ROUTE * (e - 1) + 43))
                for t in range(TPC):
                    act.wait_ge(t_xn, TPC * e + t + 1)
                    act.activation(xt_norm[:, t, :, :], out_ps[t][:, :].rearrange("p (c s) -> p c s", c=KC),
                                   ACT.Copy).then_inc(a_xn, 1)

            def beside_logits(c):
                e = chunk_due(c, 2)
                if e is None:
                    return
                act.wait_ge(t_logit, e + 1)
                act.wait_ge(d_route, due(ROUTE * (e - 1) + 2))
                act.activation(ex[:, :, :], by_expert, ACT.Exp, scale=-1.0).then_inc(a_ex, 1)

            def slot(n, j, c, g, m):
                k = n * HPG + j
                if live(k - 2):
                    sqn_high(*back(n, j, 2))
                if m is not None and j == 2:
                    keys(m)
                if m is not None and j == 3:
                    values(m)
                if (g, j) == (3, 3):
                    beside_norm(c)
                if live(k + 1):
                    wq_high(*((n, j + 1) if j < HPG - 1 else (n + 1, 0)))
                if live(k - 2):
                    wo_high(*back(n, j, 2))
                if live(k):
                    queries(n, j, g)
                if (g, j) == (0, 0):
                    beside_logits(c)
                if m is not None and j == 1:
                    turned(m)
                    keep_turned(c + 2, g, m)
                if m is not None and j == 2:
                    keys_high(m)
                if live(k - 2):
                    o_high(*back(n, j, 2))

            def attn(n, c, g, m):
                for j in range(HPG):
                    slot(n, j, c, g, m)

            walk(act, prep, attn)

        @block.vector
        def _(dve):
            def normed(m):
                dve.wait_ge(in_x, 16 * m + 16)
                dve.bn_stats(stats[:, :], x_in[:, :]).then_inc(d_stat, 1)
                dve.wait_ge(d_stat, 3 * m + 1)
                dve.wait_ge(d_xn, m)
                dve.nop(nofuse=True)
                dve.bn_aggr(mv[:, :], stats[:, :]).then_inc(d_stat, 1)
                dve.wait_ge(d_stat, 3 * m + 2)
                dve.tensor_scalar(mv[:, 1:2], mv[:, 1:2], LN_EPS, None, ALU.add).then_inc(d_stat, 1)

            def scaled(m):
                dve.wait_ge(p_rstd, m + 1)
                dve.wait_ge(t_xt, m)
                dve.tensor_scalar(xn[:, :], x_in[:, :], mv[:, 0:1], rstd[:, 0:1], ALU.subtract,
                                  ALU.mult).then_inc(d_xn, 1)

            def turned_low(m, ps=BESIDE):
                dve.wait_ge(a_xt, m + 1)
                dve.wait_ge(t_v, m)
                dve.wait_ge(a_xT, 2 * m)
                dve.tensor_tensor(xt_l[:, :, :], blocks(ps[0]), xt_h[:, :, :].bitcast(F32),
                                  ALU.subtract).then_inc(d_xt, 1)

            def keys(m):
                dve.wait_ge(a_k, 2 * m + 2)
                dve.scalar_tensor_tensor(out=sk[:, :], in0=k_exp[:, :], scalar=1.0, in1=sk[:, :],
                                         op0=ALU.min, op1=ALU.add).then_inc(d_sk, 1)

            def values_low(m, ps=BESIDE):
                dve.wait_ge(a_vh, m + 1)
                dve.wait_ge(t_kv, m)
                dve.tensor_tensor(v_l[:, :], ps[2][:, :], v_h[:, :].bitcast(F32), ALU.subtract).then_inc(d_vl, 1)

            def key_sums(m, ps=BESIDE):
                at = flat(ksum[:, ds((m // TPB) % 2), :])
                dve.wait_ge(t_ks, m + 1)
                dve.wait_ge(d_ks, m)
                dve.scalar_tensor_tensor(out=at, in0=at, scalar=keep[:, ds(m % TPB)], in1=ps[3][:, 0:2 * G:2],
                                         op0=ALU.mult, op1=ALU.add).then_inc(d_ks, 1)

            def state(m):
                at = flat(kv[:, ds((m // TPB) % 2), :])
                dve.wait_ge(t_kv, m + 1)
                dve.wait_ge(d_kv, m)
                dve.scalar_tensor_tensor(out=at, in0=at, scalar=keep[:, ds(m % TPB)], in1=m_ps[:, :],
                                         op0=ALU.mult, op1=ALU.add).then_inc(d_kv, 1)

            def queries(n, j):
                k = n * HPG + j
                dve.wait_ge(a_q, 2 * k + 2)
                dve.wait_ge(t_n, due(k - 1))
                dve.wait_ge(d_sqn, due(k - 1))
                dve.scalar_tensor_tensor(out=sq[:, j % 2, :], in0=q_exp, scalar=1.0, in1=q_pos,
                                         op0=ALU.min, op1=ALU.add).then_inc(d_sq, 1)

            def norms(n, j):
                k = n * HPG + j
                dve.wait_ge(t_n, k + 1)
                dve.wait_ge(t_b, k)
                dve.tensor_scalar(rn[:, :], n_ps[:, 0:TPC], NORM_EPS, None, ALU.add).then_inc(d_rn, 1)
                dve.wait_ge(d_rn, 2 * k + 1)
                dve.reciprocal(rn[:, :], rn[:, :]).then_inc(d_rn, 1)

            def normal(n, j):
                k = n * HPG + j
                dve.wait_ge(t_b, k + 1)
                dve.wait_ge(p_sql, k)
                dve.tensor_tensor(sqn[:, :], n_ps[:, :], sq[:, j % 2, :], ALU.mult).then_inc(d_sqn, 1)

            def o_low(n, j):
                k = n * HPG + j
                dve.wait_ge(a_oh, k + 1)
                dve.wait_ge(t_w, due(4 * (k - 1)))
                dve.tensor_tensor(o_l[:, j % 2, :], o_ps[:, :], o_h[:, j % 2, :].bitcast(F32),
                                  ALU.subtract).then_inc(d_ol, 1)

            def group_state(n, g):
                src = flat(kv[:, ds((n // TPB) % 2), ds(g * D, D)])
                dve.wait_ge(t_o, HPG * n)
                dve.wait_ge(d_kv, (n // TPB + 1) * TPB)
                dve.tensor_copy(kv_h[:, :], src).then_inc(d_kvg, 1)
                dve.wait_ge(d_kvg, 2 * n + 1)
                dve.tensor_tensor(kv_l[:, :], src, kv_h[:, :].bitcast(F32), ALU.subtract).then_inc(d_kvg, 1)

            def accumulate(n, c):
                dve.wait_ge(acc_free, 16 * c + 16)
                dve.wait_ge(d_norm, due(TPC * (c - 1)))
                for t in range(TPC):
                    at = flat(acc[:, ds(c % 2), t, :])
                    dve.wait_ge(t_w, 4 * (HPG * n + HPG - 1) + t + 1)
                    dve.wait_ge(d_acc, 4 * n)
                    dve.scalar_tensor_tensor(out=at, in0=at, scalar=keep[:, ds(n % G)], in1=out_ps[t][:, :],
                                             op0=ALU.mult, op1=ALU.add).then_inc(d_acc, 1)

            def prep(m, ahead):
                if known(m) and m == 0:
                    dve.memset(kv[:, :, :], 0.0).then_inc(d_set, 1)
                    dve.memset(ksum[:, :, :], 0.0).then_inc(d_set, 1)
                    dve.memset(earlier[:, :, :], 0.0).then_inc(d_set, 1)
                    dve.wait_ge(in_const, CONST)
                    dve.tensor_copy(ones_r[:, :], ones[:, :]).then_inc(d_set, 1)
                    dve.tensor_copy(bkv_high, bkv_raw).then_inc(d_set, 1)
                    dve.wait_ge(d_set, 5)
                    dve.tensor_tensor(bkv_low, bkv_raw, bkv_high.bitcast(F32),
                                      ALU.subtract).then_inc(d_set, 1)
                    dve.wait_ge(d_set, 6)
                    dve.tensor_scalar(bkv_raw, bkv_high.bitcast(F32), ident[0:2, 0:1],
                                      None, ALU.mult).then_inc(d_set, 1)
                    dve.wait_ge(d_set, 7)
                    for w in range(2):
                        dve.scalar_tensor_tensor(out=bkv[:, w, :], in0=bkv_low[:, w, :], scalar=ident[0:2, 1:2],
                                                 in1=bkv_raw[:, w, :], op0=ALU.mult, op1=ALU.add).then_inc(d_set, 1)
                    normed(0)
                    scaled(0)
                    dve.wait_ge(a_set, 1)
                    dve.tensor_tensor(wk_l[:, :, :], acc[:, 0, :, :], wk_h[:, :, :].bitcast(F32),
                                      ALU.subtract).then_inc(d_set, 1)
                    turned_low(0, ALONE)
                    dve.wait_ge(a_set, 2)
                    dve.tensor_tensor(wv_l[:, :, :], acc[:, 1, :, :], wv_h[:, :, :].bitcast(F32),
                                      ALU.subtract).then_inc(d_set, 1)
                    dve.wait_ge(d_set, 11)
                if ahead:
                    normed(m + 1)
                    scaled(m + 1)
                keys(m)
                values_low(m, ALONE)
                if ahead:
                    turned_low(m + 1, ALONE)
                key_sums(m, ALONE)
                state(m)

            def tile(e, t):
                return flat(acc[:, ds(e % 2), t, :])

            def statistics(e, tiles, st, steps, mv_read):
                for t in tiles:
                    if t == 0:
                        dve.wait_ge(mv_read, TPC * e)
                    if steps is d_stat1:
                        dve.wait_ge(d_acc, due(TPC * G * e + TPC * (G - 1) + t + 1))
                        dve.nop(nofuse=True)
                    else:
                        dve.wait_ge(d_mid, TPC * e + t + 1)
                        dve.nop(nofuse=True)
                    dve.bn_stats(st[:, t, :], tile(e, t)).then_inc(steps, 1)

            def aggregate(e, st, v, steps):
                dve.wait_ge(steps, STAT * e + TPC)
                dve.nop(nofuse=True)
                for t in range(TPC):
                    dve.bn_aggr(v[:, t, :], st[:, t, :]).then_inc(steps, 1)
                dve.wait_ge(steps, STAT * e + 2 * TPC)
                dve.tensor_scalar(v[:, :, 1], v[:, :, 1], LN_EPS, None, ALU.add).then_inc(steps, 1)

            def normal_output(e):
                dve.wait_ge(p_rstd1, e + 1)
                for t in range(TPC):
                    dve.tensor_scalar(tile(e, t), tile(e, t), mv1[:, t, 0:1], rstd1[:, t:t + 1],
                                      ALU.subtract, ALU.mult).then_inc(d_y, 1)

            def residual(e, tiles):
                for t in tiles:
                    dve.wait_ge(in_res[t % 2], 16 * (2 * e + t // 2 + 1))
                    dve.wait_ge(d_y, TPC * e + t + 1)
                    dve.tensor_tensor(tile(e, t), tile(e, t), x_res[:, t % 2, :], ALU.add).then_inc(d_mid, 1)

            def normal_residual(e):
                dve.wait_ge(p_rstd2, e + 1)
                dve.wait_ge(st_norm, 16 * e)
                dve.wait_ge(st_slots, 16 * TOPK * TPC * e)
                dve.wait_ge(t_xn, TPC * e)
                for t in range(TPC):
                    dve.tensor_scalar(x_norm[:, t, :], tile(e, t), mv2[:, t, 0:1], rstd2[:, t:t + 1],
                                      ALU.subtract, ALU.mult).then_inc(d_norm, 1)

            def quads(ap):
                return ap[:, :, :].rearrange("p t (g a b) -> p (t g) a b", a=2, b=2)

            def done(e, n):
                dve.wait_ge(d_route, ROUTE * e + n)

            def choose(e, part):
                if part == 0:
                    dve.wait_ge(a_ex, e + 1)
                    dve.tensor_scalar(ex[:, :, :], ex[:, :, :], 1.0, None, ALU.add).then_inc(d_route, 1)
                    done(e, 1)
                    dve.reciprocal(score[:, :, :], ex[:, :, :]).then_inc(d_route, 1)
                    done(e, 2)
                    dve.tensor_tensor(corr[:, :, :], score[:, :, :], bias[:, :, :], ALU.add).then_inc(d_route, 1)
                    done(e, 3)
                    groups = quads(corr)
                    dve.tensor_tensor(hi2[:, :, :], groups[:, :, :, 0], groups[:, :, :, 1], ALU.max).then_inc(d_route, 1)
                    dve.tensor_tensor(lo2[:, :, :], groups[:, :, :, 0], groups[:, :, :, 1], ALU.min).then_inc(d_route, 1)
                    done(e, 5)
                    dve.tensor_tensor(top[:, :], hi2[:, :, 0], hi2[:, :, 1], ALU.max).then_inc(d_route, 1)
                    dve.tensor_tensor(second[:, :], hi2[:, :, 0], hi2[:, :, 1], ALU.min).then_inc(d_route, 1)
                    dve.tensor_tensor(third[:, :], lo2[:, :, 0], lo2[:, :, 1], ALU.max).then_inc(d_route, 1)
                    done(e, 8)
                    dve.tensor_tensor(gsum[:, :], second[:, :], third[:, :], ALU.max).then_inc(d_route, 1)
                    done(e, 9)
                    dve.tensor_tensor(gsum[:, :], top[:, :], gsum[:, :], ALU.add).then_inc(d_route, 1)
                if part == 1:
                    dve.wait_ge(d_route, ROUTE * e + 10)
                    dve.nop(nofuse=True)
                    for t in range(TPC):
                        dve.max(g8[:, t, :], gsum[:, t * NG:(t + 1) * NG]).then_inc(d_route, 1)
                    dve.wait_ge(d_route, ROUTE * e + 14)
                    dve.nop(nofuse=True)
                    for t in range(TPC):
                        dve.max_index(gi[:, t, :], g8[:, t, :], gsum[:, t * NG:(t + 1) * NG]).then_inc(d_route, 1)
                    done(e, 18)
                    dve.tensor_tensor(g_hot[:, :, :, :], iota_g[:, :, :].rearrange("p (t g) k -> p t g k", t=TPC),
                                      gi[:, :, 0:TOPG].rearrange("p t (a k) -> p t a k", a=1).to_broadcast(
                                          [P, TPC, NG, TOPG]), ALU.is_equal).then_inc(d_route, 1)
                    done(e, 19)
                    dve.tensor_reduce(gmask[:, :], g_hot[:, :, :, :].rearrange("p t g k -> p (t g) k"), AX.X,
                                      ALU.add).then_inc(d_route, 1)
                    done(e, 20)
                    dve.tensor_tensor(masked[:, :, :].rearrange("p t (g e) -> p (t g) e", g=NG),
                                      corr[:, :, :].rearrange("p t (g e) -> p (t g) e", g=NG),
                                      gmask[:, :].rearrange("p (g a) -> p g a", a=1).to_broadcast([P, TPC * NG, EPG]),
                                      ALU.mult).then_inc(d_route, 1)
                if part == 2:
                    dve.wait_ge(d_route, ROUTE * e + 21)
                    dve.nop(nofuse=True)
                    for t in range(TPC):
                        dve.max(e8[:, t, :], masked[:, t, :]).then_inc(d_route, 1)
                    dve.wait_ge(d_route, ROUTE * e + 25)
                    dve.nop(nofuse=True)
                    for t in range(TPC):
                        dve.max_index(ei[:, t, :], e8[:, t, :], masked[:, t, :]).then_inc(d_route, 1)
                    done(e, 29)
                    dve.tensor_tensor(hot[:, :, :, :], iota[:, :, :].rearrange("p (t k) e -> p t k e", t=TPC),
                                      ei[:, :, 0:TOPK].rearrange("p t (k a) -> p t k a", a=1).to_broadcast(
                                          [P, TPC, TOPK, NE]), ALU.is_equal).then_inc(d_route, 1)
                    done(e, 30)
                    dve.tensor_reduce(chosen[:, :, :], hot[:, :, :, :].rearrange("p t k e -> p t e k"), AX.X,
                                      ALU.add).then_inc(d_route, 1)
                    for t in range(1, TPC):
                        done(e, CHOSEN + t - 1)
                        dve.tensor_tensor(earlier[:, t, :], earlier[:, t - 1, :], chosen[:, t - 1, :],
                                          ALU.add).then_inc(d_route, 1)

            def count_earlier(e):
                dve.wait_ge(t_place, e + 1)
                dve.tensor_tensor(hot_part, hot[:, :, :, :],
                                  by_expert.rearrange("p t (a e) -> p t a e", a=1).to_broadcast(
                                      [P, TPC, TOPK, NE]), ALU.mult).then_inc(d_route, 1)
                done(e, 35)
                dve.tensor_reduce(place[:, :, :], hot_part, AX.X, ALU.add).then_inc(d_route, 1)
                dve.tensor_tensor(earlier[:, 0, :], earlier[:, TPC - 1, :], chosen[:, TPC - 1, :],
                                  ALU.add).then_inc(d_route, 1)

            def slots_and_weights(e):
                done(e, PLACED)
                dve.tensor_scalar(over[:, :, :], place[:, :, :], float(CAP), SKIP, ALU.is_ge,
                                  ALU.mult).then_inc(d_route, 1)
                dve.scalar_tensor_tensor(out=slot_f[:, :, :], in0=ei[:, :, 0:TOPK], scalar=float(CAP),
                                         in1=place[:, :, :], op0=ALU.mult, op1=ALU.add).then_inc(d_route, 1)
                dve.tensor_scalar(fits[:, :, :], place[:, :, :], float(CAP), None, ALU.is_lt).then_inc(d_route, 1)
                done(e, 40)
                dve.wait_ge(st_slots, 16 * TOPK * TPC * e)
                dve.tensor_tensor(slot_of[:, :, :], slot_f[:, :, :], over[:, :, :], ALU.add).then_inc(d_route, 1)
                dve.tensor_tensor(hot_part, hot[:, :, :, :],
                                  score[:, :, :].rearrange("p t (a e) -> p t a e", a=1).to_broadcast(
                                      [P, TPC, TOPK, NE]), ALU.mult).then_inc(d_route, 1)
                done(e, 42)
                dve.tensor_reduce(weight[:, :, :], hot_part, AX.X, ALU.add).then_inc(d_route, 1)
                done(e, 43)
                dve.tensor_reduce(wsum[:, :], weight[:, :, :], AX.X, ALU.add).then_inc(d_route, 1)
                done(e, 44)
                dve.tensor_scalar(wsum[:, :], wsum[:, :], 1e-20, None, ALU.add).then_inc(d_route, 1)
                done(e, 45)
                dve.reciprocal(winv[:, :], wsum[:, :]).then_inc(d_route, 1)
                done(e, 46)
                dve.scalar_tensor_tensor(out=weight[:, :, :], in0=weight[:, :, :], scalar=SCALE,
                                         in1=winv[:, :].rearrange("p (t a) -> p t a", a=1).to_broadcast([P, TPC, TOPK]),
                                         op0=ALU.mult, op1=ALU.mult).then_inc(d_route, 1)
                done(e, 47)
                dve.tensor_tensor(weight_all[:, ds(e * TPC, TPC), :], weight[:, :, :], fits[:, :, :],
                                  ALU.mult).then_inc(d_route, 1)
                dve.tensor_copy(slot_all[:, ds(e * TPC, TPC), :], slot_of[:, :, :]).then_inc(d_route, 1)

            def beside(c, g, j):
                e = chunk_due(c, 1)
                if e is not None:
                    if (g, j) == (1, 0):
                        statistics(e, range(TPC), stats1, d_stat1, d_y)
                    if (g, j) == (1, 1):
                        aggregate(e, stats1, mv1, d_stat1)
                    if (g, j) == (1, 3):
                        normal_output(e)
                    if (g, j) == (2, 0):
                        residual(e, (0, 1))
                    if (g, j) == (2, 1):
                        statistics(e, (0, 1), stats2, d_stat2, d_norm)
                        residual(e, (2, 3))
                    if (g, j) == (2, 3):
                        statistics(e, (2, 3), stats2, d_stat2, d_norm)
                        aggregate(e, stats2, mv2, d_stat2)
                    if (g, j) == (3, 0):
                        normal_residual(e)
                e = chunk_due(c, 2)
                if e is not None:
                    if g == 0 and j >= 1:
                        choose(e, j - 1)
                    if (g, j) == (1, 0):
                        count_earlier(e)
                    if (g, j) == (1, 1):
                        slots_and_weights(e)

            def slot(n, j, c, g, m):
                k = n * HPG + j
                if live(k - 2):
                    normal(*back(n, j, 2))
                if m is not None and j == 0:
                    normed(m)
                if m is not None and j == 3:
                    values_low(m)
                if live(k - 1):
                    norms(*back(n, j, 1))
                if m is not None and j == 1:
                    turned_low(m)
                if live(k):
                    queries(n, j)
                if m is not None and j == 0:
                    scaled(m)
                if m is not None and j == 2:
                    keys(m)
                if m is not None and j == 3:
                    key_sums(m)
                if j == 2 and live(k - 3):
                    accumulate(n - 1, c if g else c - 1)
                beside(c, g, j)
                if m is not None and j == 3:
                    state(m)
                if live(k - 2):
                    o_low(*back(n, j, 2))
                if j == 1 and live(k):
                    group_state(n, g)

            def attn(n, c, g, m):
                for j in range(HPG):
                    slot(n, j, c, g, m)

            walk(dve, prep, attn)

        @block.tensor
        def _(pe):
            def turn(m, ps=BESIDE):
                pe.wait_ge(d_xn, m + 1)
                if ps is BESIDE:
                    pe.wait_ge(d_kv, m)
                else:
                    pe.wait_ge(d_xt, m)
                for b in range(KC):
                    last = pe.transpose(blocks(ps[0])[:, b, :], xn[:, b * P:(b + 1) * P], ident[:, :])
                last.then_inc(t_xt, 1)

            def project(out, w_h, w_l, bias):
                pe.matmul(out[:, :], ones_r[0:2, :], bkv[:, bias, :], start=True, stop=False,
                          skip_group_check=True)
                for b in range(KC):
                    last = three(pe, out[:, :], (xt_h[:, b, :], xt_l[:, b, :]), (w_h[:, b, :], w_l[:, b, :]),
                                 first=False, last=b == KC - 1)
                return last

            def keys(m, ps=BESIDE):
                pe.wait_ge(d_xt, m + 1)
                pe.wait_ge(a_k, 2 * m)
                project(ps[1], wk_h, wk_l, 0).then_inc(t_k, 1)

            def values(m, ps=BESIDE):
                if ps is BESIDE:
                    pe.wait_ge(a_k, 2 * m + 2)
                else:
                    pe.wait_ge(d_vl, m)
                project(ps[2], wv_h, wv_l, 1).then_inc(t_v, 1)

            def key_sums(m, ps=BESIDE):
                pe.wait_ge(p_skl, m + 1)
                if ps is BESIDE:
                    pe.wait_ge(d_vl, m + 1)
                else:
                    pe.wait_ge(d_ks, m)
                for g in range(G):
                    at = ds(g * D, D)
                    pe.matmul(ps[3][:, 2 * g:2 * g + 2], sk_h[:, at], ones_r[:, 0:2], start=True, stop=False,
                              skip_group_check=True)
                    last = pe.matmul(ps[3][:, 2 * g:2 * g + 2], sk_l[:, at], ones_r[:, 0:2], start=False,
                                     stop=True, skip_group_check=True)
                last.then_inc(t_ks, 1)

            def key_values(m, ps=BESIDE):
                if ps is BESIDE:
                    pe.wait_ge(d_ks, m + 1)
                else:
                    pe.wait_ge(d_vl, m + 1)
                    pe.wait_ge(d_kv, m)
                for g in range(G):
                    at = ds(g * D, D)
                    last = three(pe, m_ps[:, at], (sk_h[:, at], sk_l[:, at]), (v_h[:, at], v_l[:, at]))
                last.then_inc(t_kv, 1)

            def query(n, j, c):
                k = n * HPG + j
                r, at = j % 2, ds(c % 3)
                pe.wait_ge(p_wq, k + 1)
                pe.wait_ge(a_q, 2 * k)
                if j == 0:
                    pe.wait_ge(a_xT, 2 * (c + 1) * TPC)
                for b in range(KC):
                    last = three(pe, q_ps[:, :], (wq_h[:, r, b, :], wq_l[:, r, b, :]),
                                 (xT_h[:, at, b, :].rearrange("p a s -> p (a s)"),
                                  xT_l[:, at, b, :].rearrange("p a s -> p (a s)")),
                                 first=b == 0, last=b == KC - 1)
                last.then_inc(t_q, 1)

            def norm(n, j):
                k = n * HPG + j
                sums = ksum[:, ds((n // TPB) % 2), ds(n % G)].rearrange("p a s -> p (a s)")
                pe.wait_ge(d_sq, k + 1)
                pe.wait_ge(d_sqn, k)
                pe.wait_ge(d_ks, (n // TPB + 1) * TPB)
                for t in range(TPC):
                    last = pe.matmul(n_ps[:, t:t + 1], sq[:, j % 2, t * P:(t + 1) * P], sums, start=True,
                                     stop=True, skip_group_check=True)
                last.then_inc(t_n, 1)

            def spread(n, j):
                k = n * HPG + j
                pe.wait_ge(d_rn, 2 * k + 2)
                for t in range(TPC):
                    last = pe.transpose(n_ps[:, t * P:(t + 1) * P], rn[:, t:t + 1].to_broadcast([P, P]),
                                        ident[:, :])
                last.then_inc(t_b, 1)

            def attend(n, j):
                k = n * HPG + j
                pe.wait_ge(p_sql, k + 1)
                pe.wait_ge(d_kvg, 2 * n + 2)
                pe.wait_ge(d_ol, k)
                three(pe, o_ps[:, :], (kv_h[:, :], kv_l[:, :]), (sqn_h[:, :], sqn_l[:, :])).then_inc(t_o, 1)

            def output(n, j, turned_chunk):
                k = n * HPG + j
                pe.wait_ge(d_ol, k + 1)
                pe.wait_ge(p_wo, k + 1)
                for t in range(TPC):
                    if j == 0:
                        pe.wait_ge(d_acc, due(4 * (n - 1) + t + 1))
                    if j == 0 and turned_chunk is not None:
                        pe.wait_ge(a_xn, TPC * turned_chunk + t + 1)
                    at = ds(t * P, P)
                    three(pe, out_ps[t][:, :], (o_h[:, j % 2, at], o_l[:, j % 2, at]),
                          (wo_h[:, j % 2, :], wo_l[:, j % 2, :]), first=j == 0,
                          last=j == HPG - 1).then_inc(t_w, 1)

            def prep(m, ahead):
                if known(m) and m == 0:
                    pe.wait_ge(d_set, 4)
                    pe.wait_ge(in_const, CONST)
                    turn(0, ALONE)
                    pe.wait_ge(d_set, 10)
                keys(m, ALONE)
                if ahead:
                    turn(m + 1, ALONE)
                if known(m) and m == 0:
                    pe.wait_ge(d_set, 11)
                values(m, ALONE)
                key_sums(m, ALONE)
                key_values(m, ALONE)

            def steps_done(n):
                return min(n, NT) if known(n) else n

            def turn_norm(e, n):
                for t in range(TPC):
                    pe.wait_ge(d_norm, TPC * e + t + 1)
                    pe.wait_ge(d_acc, TPC * steps_done(n))
                    for b in range(KC):
                        last = pe.transpose(out_ps[t][:, b * P:(b + 1) * P], x_norm[:, t, b * P:(b + 1) * P],
                                            ident[:, :])
                    last.then_inc(t_xn, 1)

            def logits(e, m):
                pe.wait_ge(a_xn, TPC * (e + 1))
                pe.wait_ge(d_kv, NT if m is None else m)
                for t in range(TPC):
                    for b in range(KC):
                        last = pe.matmul(by_expert[:, t, :], xt_norm[:, t, b, :], gate[:, b, :], start=b == 0,
                                         stop=b == KC - 1, skip_group_check=True)
                last.then_inc(t_logit, 1)

            def places(e, m):
                pe.wait_ge(d_route, ROUTE * e + PRIOR)
                pe.wait_ge(d_kv, NT if m is None else m)
                pe.matmul(by_expert, before_me[:, :], chosen[:, :, :], start=True, stop=False,
                          skip_group_check=True)
                pe.matmul(by_expert, ones[:, :], earlier[:, :, :], start=False, stop=True,
                          skip_group_check=True).then_inc(t_place, 1)

            def slot(n, j, c, g, m):
                k = n * HPG + j
                e1, e2 = chunk_due(c, 1), chunk_due(c, 2)
                if live(k):
                    query(n, j, c)
                if live(k - 1):
                    norm(*back(n, j, 1))
                if e1 is not None and (g, j) == (3, 3):
                    turn_norm(e1, n)
                if e2 is not None and (g, j) == (1, 0):
                    places(e2, m)
                if m is not None and j == 1:
                    if e2 is not None and g == 0:
                        pe.wait_ge(a_ex, e2 + 1)
                    if e2 is not None and g == 1:
                        pe.wait_ge(d_route, ROUTE * e2 + CHOSEN + 4)
                    turn(m)
                if m is not None and j == 3:
                    key_sums(m)
                if live(k - 3):
                    output(*back(n, j, 3), e1 if g == 3 else None)
                if e2 is not None and (g, j) == (0, 0):
                    logits(e2, m)
                if m is not None and j == 3:
                    key_values(m)
                if live(k - 2):
                    attend(*back(n, j, 2))
                if live(k - 1):
                    spread(*back(n, j, 1))
                if m is not None and j == 1:
                    keys(m)
                if m is not None and j == 2:
                    values(m)

            def attn(n, c, g, m):
                for j in range(HPG):
                    slot(n, j, c, g, m)

            walk(pe, prep, attn)


def phase_experts(nc, d, slots, rows):
    FB = FE // P
    SB = CAP // P
    with ExitStack() as ctx:
        def sb(name, shape, dt=F32):
            return ctx.enter_context(nc.sbuf_tensor("e_" + name, shape, dt))

        def sem(name):
            return ctx.enter_context(nc.semaphore("e_" + name))

        def bank(name):
            return ctx.enter_context(nc.psum_tensor("e_" + name, [P, 512], F32))

        ident = sb("ident", [P, P])
        x_in = sb("x_in", [P, 2, SB, C])
        up, up_h, up_l = sb("up", [P, 2, KC * FE]), sb("up_h", [P, 2, KC * FE], F32R), sb("up_l", [P, 2, KC * FE], F32R)
        down, down_h, down_l = sb("down", [P, 2, FB * C]), sb("down_h", [P, 2, FB * C], F32R), sb("down_l", [P, 2, FB * C], F32R)
        xt_h, xt_l = sb("xt_h", [P, 2, KC, CAP], F32R), sb("xt_l", [P, 2, KC, CAP], F32R)
        relu, hid = sb("relu", [P, FB * CAP]), sb("hid", [P, FB * CAP])
        hid_h, hid_l = sb("hid_h", [P, 2, FB, CAP], F32R), sb("hid_l", [P, 2, FB, CAP], F32R)
        y = sb("y", [P, 2, SB, C])
        turn_ps = [bank(f"turn_ps{i}") for i in range(2)]
        up_ps = [bank(f"up_ps{i}") for i in range(2)]
        down_ps = [bank(f"down_ps{i}") for i in range(4)]

        in_const = sem("in_const")
        in_x, in_up, in_down = ([sem(f"{n}{i}") for i in range(2)] for n in ("in_x", "in_up", "in_down"))
        t_xt, a_xt, d_xt = sem("t_xt"), sem("a_xt"), sem("d_xt")
        d_up, p_up, a_down, p_down = sem("d_up"), sem("p_up"), sem("a_down"), sem("p_down")
        t_up, a_relu, d_hid, a_hid, d_hidl = sem("t_up"), sem("a_relu"), sem("d_hid"), sem("a_hid"), sem("d_hidl")
        t_down, a_y, d_y = sem("t_down"), sem("a_y"), sem("d_y")
        st_y = [sem(f"st_y{i}") for i in range(2)]
        block = ctx.enter_context(nc.Block())

        def walk(eng, slot, lag):
            for e in range(4):
                slot(e, e % 2, e // 2)
            with eng.Fori(2, NE // 2) as i:
                slot(2 * i, 0, i)
                slot(2 * i + 1, 1, i)
            for e in range(NE, NE + lag):
                slot(e, e % 2, e // 2)

        def live(e, lag=0):
            return not known(e) or 0 <= e - lag < NE

        @block.sync
        def _(sp):
            sp.dma_start(ident[:, :], d["ident"]).then_inc(in_const, 16)

            def slot(e, r, i):
                if live(e):
                    sp.wait_ge(t_xt, due(2 * (e - 1)))
                    sp.dma_start(x_in[:, r, :, :], slots[ds(e * CAP, CAP), :].rearrange(
                        "(s p) c -> p s c", p=P)).then_inc(in_x[r], 16)
                    sp.wait_ge(d_up, due(e - 1))
                    sp.wait_ge(p_up, due(e - 1))
                    sp.dma_start(up[:, r, :], d["up"][ds(e), :, :].rearrange("a p n -> (a p) n")).then_inc(in_up[r], 16)
                    sp.wait_ge(a_down, due(e - 1))
                    sp.wait_ge(p_down, due(e - 1))
                    sp.dma_start(down[:, r, :], d["down"][ds(e), :, :].rearrange("a p n -> (a p) n")).then_inc(in_down[r], 16)
            walk(sp, slot, 0)

        @block.gpsimd
        def _(pool):
            def slot(e, r, i):
                if live(e):
                    pool.wait_ge(d_up, e + 1)
                    pool.wait_ge(t_up, due(e - 1))
                    pool.tensor_tensor(up_l[:, r, :], up[:, r, :], up_h[:, r, :].bitcast(F32),
                                       ALU.subtract).then_inc(p_up, 1)
                    pool.wait_ge(a_down, e + 1)
                    pool.wait_ge(t_down, due(2 * (e - 1)))
                    pool.tensor_tensor(down_l[:, r, :], down[:, r, :], down_h[:, r, :].bitcast(F32),
                                       ALU.subtract).then_inc(p_down, 1)
            walk(pool, slot, 0)

        @block.scalar
        def _(act):
            def slot(e, r, i):
                q = 1 - r
                if live(e, 3):
                    act.wait_ge(a_y, due(e - 2))
                    act.wait_ge(d_y, due(e - 2))
                    act.dma_start(rows[ds((e - 3) * CAP, CAP), :].rearrange("(s p) c -> p s c", p=P),
                                  y[:, q, :, :]).then_inc(st_y[q], 16)
                if live(e):
                    for b in range(2):
                        act.wait_ge(t_xt, 2 * e + b + 1)
                        if b == 0:
                            act.wait_ge(t_up, due(e - 1))
                        act.activation(xt_h[:, r, 2 * b:2 * b + 2, :],
                                       turn_ps[b][:, :].rearrange("p (c s) -> p c s", c=2),
                                       ACT.Copy).then_inc(a_xt, 1)
                    act.wait_ge(in_down[r], 16 * i + 16)
                    act.wait_ge(t_down, due(2 * (e - 1)))
                    act.wait_ge(p_down, due(e - 1))
                    act.activation(down_h[:, r, :], down[:, r, :], ACT.Copy).then_inc(a_down, 1)
                if live(e, 1):
                    act.wait_ge(t_up, e)
                    act.wait_ge(d_hid, due(e - 1))
                    act.activation(relu[:, :], up_ps[q][:, :], ACT.Relu).then_inc(a_relu, 1)
                    act.wait_ge(d_hid, e)
                    act.wait_ge(t_down, due(2 * (e - 2)))
                    act.activation(hid_h[:, q, :, :].rearrange("p a b -> p (a b)"), hid[:, :],
                                   ACT.Copy).then_inc(a_hid, 1)
                if live(e, 2):
                    act.wait_ge(t_down, due(2 * (e - 2) + 1))
                    act.wait_ge(st_y[r], due(16 * (i - 1)))
                    act.activation(y[:, r, 0, :], down_ps[2 * r][:, :], ACT.Copy).then_inc(a_y, 1)
            walk(act, slot, 3)
            for r in range(2):
                act.wait_ge(st_y[r], 16 * (NE // 2))

        @block.vector
        def _(dve):
            def slot(e, r, i):
                q = 1 - r
                if live(e):
                    dve.wait_ge(in_up[r], 16 * i + 16)
                    dve.wait_ge(t_up, due(e - 1))
                    dve.wait_ge(p_up, due(e - 1))
                    dve.tensor_copy(up_h[:, r, :], up[:, r, :]).then_inc(d_up, 1)
                    for b in range(2):
                        dve.wait_ge(a_xt, 2 * e + b + 1)
                        dve.tensor_tensor(xt_l[:, r, 2 * b:2 * b + 2, :],
                                          turn_ps[b][:, :].rearrange("p (c s) -> p c s", c=2),
                                          xt_h[:, r, 2 * b:2 * b + 2, :].bitcast(F32),
                                          ALU.subtract).then_inc(d_xt, 1)
                if live(e, 1):
                    dve.wait_ge(a_relu, e)
                    dve.wait_ge(a_hid, due(e - 1))
                    dve.wait_ge(d_hidl, due(e - 1))
                    dve.scalar_tensor_tensor(out=hid[:, :], in0=up_ps[q][:, :], scalar=0.0, in1=relu[:, :],
                                             op0=ALU.max, op1=ALU.mult).then_inc(d_hid, 1)
                    dve.wait_ge(a_hid, e)
                    dve.tensor_tensor(hid_l[:, q, :, :].rearrange("p a b -> p (a b)"), hid[:, :],
                                      hid_h[:, q, :, :].rearrange("p a b -> p (a b)").bitcast(F32),
                                      ALU.subtract).then_inc(d_hidl, 1)
                if live(e, 2):
                    dve.wait_ge(t_down, due(2 * (e - 2) + 2))
                    dve.wait_ge(st_y[r], due(16 * (i - 1)))
                    dve.tensor_copy(y[:, r, 1, :], down_ps[2 * r + 1][:, :]).then_inc(d_y, 1)
            walk(dve, slot, 2)

        @block.tensor
        def _(pe):
            pe.wait_ge(in_const, 16)

            def slot(e, r, i):
                q = 1 - r
                if live(e):
                    pe.wait_ge(in_x[r], 16 * i + 16)
                    for b in range(KC):
                        if b % 2 == 0:
                            pe.wait_ge(d_xt, due(2 * (e - 1) + b // 2 + 1))
                        for s in range(SB):
                            last = pe.transpose(turn_ps[b // 2][:, (b % 2) * CAP + s * P:(b % 2) * CAP + (s + 1) * P],
                                                x_in[:, r, s, b * P:(b + 1) * P], ident[:, :])
                        if b % 2 == 1:
                            last.then_inc(t_xt, 1)
                if live(e, 1):
                    pe.wait_ge(d_xt, 2 * e)
                    pe.wait_ge(p_up, e)
                    pe.wait_ge(d_hid, due(e - 2))
                    for f in range(FB):
                        out = up_ps[q][:, f * CAP:(f + 1) * CAP]
                        for b in range(KC):
                            at = ds(b * FE + f * P, P)
                            last = three(pe, out, (up_h[:, q, at], up_l[:, q, at]),
                                         (xt_h[:, q, b, :], xt_l[:, q, b, :]), first=b == 0, last=b == KC - 1)
                    last.then_inc(t_up, 1)
                if live(e, 2):
                    pe.wait_ge(d_hidl, due(e - 1))
                    pe.wait_ge(p_down, due(e - 1))
                    for s in range(SB):
                        pe.wait_ge((a_y, d_y)[s], due(e - 3))
                        for f in range(FB):
                            at, to = ds(s * P, P), ds(f * C, C)
                            last = three(pe, down_ps[2 * r + s][:, :], (hid_h[:, r, f, at], hid_l[:, r, f, at]),
                                         (down_h[:, r, to], down_l[:, r, to]), first=f == 0, last=f == FB - 1)
                        last.then_inc(t_down, 1)
            walk(pe, slot, 2)


def phase_shared(nc, d, x1, x2, rows, kept, out):
    slot_all, weight_all = kept
    FB = FS // P
    with ExitStack() as ctx:
        def sb(name, shape, dt=F32):
            return ctx.enter_context(nc.sbuf_tensor("s_" + name, shape, dt))

        def sem(name):
            return ctx.enter_context(nc.semaphore("s_" + name))

        def bank(name):
            return ctx.enter_context(nc.psum_tensor("s_" + name, [P, 512], F32))

        ident, power = sb("ident", [P, P]), sb("power", [P, 1])
        raw = sb("raw", [P, KC * FS])
        up_h, up_l = sb("up_h", [P, KC, FS], F32R), sb("up_l", [P, KC, FS], F32R)
        down_h, down_l = sb("down_h", [P, FB, C], F32R), sb("down_l", [P, FB, C], F32R)
        x_in = sb("x_in", [P, 2, C])
        xt_h, xt_l = sb("xt_h", [P, 2, KC, CH], F32R), sb("xt_l", [P, 2, KC, CH], F32R)
        relu, hid = sb("relu", [P, CH]), sb("hid", [P, CH])
        hid_h, hid_l = sb("hid_h", [P, 2, CH], F32R), sb("hid_l", [P, 2, CH], F32R)
        got = sb("got", [P, 2, TOPK, C])
        slot = sb("slot", [P, TPC, TOPK], U32)
        y, x_mid, z = sb("y", [P, TPC, C]), sb("x_mid", [P, 2, C]), sb("z", [P, 2, C])
        stats, mv, rstd = sb("stats", [P, 6]), sb("mv", [P, 2]), sb("rstd", [P, 1])
        turn_ps = bank("turn_ps")
        up_ps = [bank(f"up_ps{i}") for i in range(2)]
        down_ps = [bank(f"down_ps{t}") for t in range(TPC)]

        in_const, in_raw, in_x2 = sem("in_const"), sem("in_raw"), sem("in_x2")
        in_x1 = [sem(f"in_x1{i}") for i in range(2)]
        in_rows, st_out = [sem(f"in_rows{i}") for i in range(2)], [sem(f"st_out{i}") for i in range(2)]
        p_set, a_set, d_set = sem("p_set"), sem("a_set"), sem("d_set")
        t_xt, a_xt, d_xt = sem("t_xt"), sem("a_xt"), sem("d_xt")
        t_up, a_relu, a_sq, a_hid, d_hid = sem("t_up"), sem("a_relu"), sem("a_sq"), sem("a_hid"), sem("d_hid")
        t_down, d_slot = sem("t_down"), sem("d_slot")
        a_first, d_sum, d_stat, p_rstd, d_z, d_out = (sem(n) for n in ("a_first", "d_sum", "d_stat", "p_rstd", "d_z", "d_out"))
        block = ctx.enter_context(nc.Block())

        def walk(eng, before, slot, after):
            before()
            for c in range(2):
                for f in range(FB):
                    slot(c, f)
            with eng.Fori(2, NCH) as c:
                for f in range(FB):
                    slot(c, f)
            after()

        def tile_due(c, f):
            owner, t = (c - 1, f // 2 - 1) if f >= 2 else (c - 2, TPC - 1)
            return (owner, t) if not known(c) or owner >= 0 else None

        def gather_due(c, f):
            if f % 2 == 0:
                return None
            owner, t = (c, 0) if f == FB - 1 else (c - 1, f // 2 + 1)
            return (owner, t) if not known(c) or owner >= 0 else None

        def back2(c, f):
            return (c, f - 2) if f >= 2 else (c - 1, f - 2 + FB)

        @block.sync
        def _(sp):
            sp.dma_start(ident[:, :], d["ident"]).then_inc(in_const, 16)
            sp.dma_start(raw[:, :], d["shared_up"]).then_inc(in_raw, 16)

            def load_x2(t, r):
                sp.wait_ge(t_xt, due(t - 1))
                sp.wait_ge(in_x2, 16 * t)
                sp.dma_start(x_in[:, r, :], x2[ds(t % NT), :, :].rearrange("a p c -> (a p) c")).then_inc(in_x2, 16)

            def before():
                load_x2(0, 0)
                sp.wait_ge(d_set, 1)
                sp.dma_start(raw[:, :], d["shared_down"]).then_inc(in_raw, 16)
                for t in range(1, TPC + 1):
                    load_x2(t, t % 2)

            def residual(c, t):
                n, r = c * TPC + t, t % 2
                sp.wait_ge(d_out, due(n - 1))
                sp.dma_start(x_mid[:, r, :], x1[ds(n), :, :].rearrange("a p c -> (a p) c")).then_inc(in_x1[r], 16)

            def result(c, t):
                n, r = c * TPC + t, t % 2
                sp.wait_ge(d_out, n + 1)
                sp.dma_start(out[ds(n), :, :].rearrange("a p c -> (a p) c"), z[:, r, :]).then_inc(st_out[r], 16)

            def slot(c, f):
                if f % 2 == 0:
                    load_x2(c * TPC + TPC + f // 2 + 1, (f // 2 + 1) % 2)
                if f % 2 == 0:
                    if tile_due(c, f):
                        residual(*tile_due(c, f))
                    before = tile_due(c, f - 2) if f >= 2 else tile_due(c - 1, FB - 1)
                    if before:
                        result(*before)

            def after():
                residual(NCH - 2, TPC - 1)
                result(NCH - 2, TPC - 2)
                residual(NCH - 1, 0)
                result(NCH - 2, TPC - 1)
                for t in range(TPC):
                    if t + 1 < TPC:
                        residual(NCH - 1, t + 1)
                    result(NCH - 1, t)
                for r in range(2):
                    sp.wait_ge(st_out[r], 16 * NT // 2)
                sp.wait_ge(in_x2, 16 * (NT + TPC + 1))
            walk(sp, before, slot, after)

        @block.gpsimd
        def _(pool):
            pool.memset(power[:, :], -0.5).then_inc(p_set, 1)
            pool.memset(got[:, :, :, :], 0.0).then_inc(p_set, 1)
            pool.wait_ge(p_set, 2)

            def gather(c, t):
                n, r = c * TPC + t, t % 2
                pool.wait_ge(d_slot, c + 1)
                pool.wait_ge(d_sum, due(TOPK * (n - 1)))
                pool.nop(nofuse=True)
                for k in range(TOPK):
                    pool.indirect_dma_start(got[:, r, k, :], None, rows,
                                            bass.IndirectOffsetOnAxis(ap=slot[:, t, k:k + 1], axis=0),
                                            bounds_check=NSLOT - 1, oob_is_err=False).then_inc(in_rows[r], 16)

            def deviation(c, t):
                n = c * TPC + t
                pool.wait_ge(d_stat, 3 * n + 3)
                pool.wait_ge(d_z, n)
                pool.tensor_tensor(rstd[:, :], mv[:, 1:2], power[:, :], ALU.pow).then_inc(p_rstd, 1)

            def slot_work(c, f):
                if f % 2 == 1 and tile_due(c, f):
                    deviation(*tile_due(c, f))
                if gather_due(c, f):
                    gather(*gather_due(c, f))

            def after():
                gather(NCH - 1, 1)
                deviation(NCH - 2, TPC - 1)
                for t in range(TPC):
                    if t < 2:
                        gather(NCH - 1, t + 2)
                    deviation(NCH - 1, t)
            walk(pool, lambda: None, slot_work, after)
            for r in range(2):
                pool.wait_ge(in_rows[r], 16 * TOPK * NT // 2)

        @block.scalar
        def _(act):
            def turned(c, t):
                n = c * TPC + t
                act.wait_ge(t_xt, n + 1)
                act.activation(xt_h[:, ds(c % 2), :, ds(t * P, P)].rearrange("p a c s -> p (a c) s"),
                               turn_ps[:, :].rearrange("p (c s) -> p c s", c=KC), ACT.Copy).then_inc(a_xt, 1)

            def before():
                act.wait_ge(in_raw, 16)
                act.activation(up_h[:, :, :].rearrange("p a b -> p (a b)"), raw[:, :], ACT.Copy).then_inc(a_set, 1)
                for t in range(TPC):
                    turned(0, t)
                act.wait_ge(in_raw, 32)
                act.activation(down_h[:, :, :].rearrange("p a b -> p (a b)"), raw[:, :], ACT.Copy).then_inc(a_set, 1)

            def hidden(c, f):
                k = c * FB + f
                act.wait_ge(t_up, k + 1)
                act.wait_ge(a_sq, k)
                act.activation(relu[:, :], up_ps[f % 2][:, :], ACT.Relu).then_inc(a_relu, 1)
                act.wait_ge(a_relu, k + 1)
                act.wait_ge(a_hid, k)
                act.wait_ge(d_hid, k)
                act.activation(hid[:, :], relu[:, :], ACT.Square).then_inc(a_sq, 1)
                act.wait_ge(a_sq, k + 1)
                act.wait_ge(t_down, due(TPC * (k - 1)))
                act.activation(hid_h[:, f % 2, :], hid[:, :], ACT.Copy).then_inc(a_hid, 1)

            def empty_bank(c, t):
                n = c * TPC + t
                act.wait_ge(t_down, due(TPC * (c * FB + FB - 1) + t + 1))
                act.wait_ge(d_z, due(n - TPC + 1))
                act.activation(y[:, t, :], down_ps[t][:, :], ACT.Copy).then_inc(a_first, 1)

            def slot(c, f):
                hidden(c, f)
                if f % 2 == 0:
                    turned(c + 1, f // 2)
                if f == 1 and (not known(c) or c > 0):
                    for t in range(TPC):
                        empty_bank(c - 1, t)

            def after():
                for t in range(TPC):
                    empty_bank(NCH - 1, t)
            walk(act, before, slot, after)

        @block.vector
        def _(dve):
            def turned(c, t):
                n = c * TPC + t
                at = (slice(None), ds(c % 2), slice(None), ds(t * P, P))
                dve.wait_ge(a_xt, n + 1)
                dve.tensor_tensor(xt_l[at].rearrange("p a c s -> p (a c) s"),
                                  turn_ps[:, :].rearrange("p (c s) -> p c s", c=KC),
                                  xt_h[at].rearrange("p a c s -> p (a c) s").bitcast(F32),
                                  ALU.subtract).then_inc(d_xt, 1)

            def before():
                dve.wait_ge(a_set, 1)
                dve.tensor_tensor(up_l[:, :, :].rearrange("p a b -> p (a b)"), raw[:, :],
                                  up_h[:, :, :].rearrange("p a b -> p (a b)").bitcast(F32),
                                  ALU.subtract).then_inc(d_set, 1)
                for t in range(TPC):
                    turned(0, t)
                dve.wait_ge(a_set, 2)
                dve.tensor_tensor(down_l[:, :, :].rearrange("p a b -> p (a b)"), raw[:, :],
                                  down_h[:, :, :].rearrange("p a b -> p (a b)").bitcast(F32),
                                  ALU.subtract).then_inc(d_set, 1)

            def hid_low(c, f):
                k = c * FB + f
                dve.wait_ge(a_hid, k + 1)
                dve.wait_ge(t_down, due(TPC * (k - 1)))
                dve.tensor_tensor(hid_l[:, f % 2, :], hid[:, :], hid_h[:, f % 2, :].bitcast(F32),
                                  ALU.subtract).then_inc(d_hid, 1)

            def add_rows(c, t):
                n, r = c * TPC + t, t % 2
                i = c * (TPC // 2) + t // 2
                dve.wait_ge(in_rows[r], 16 * TOPK * (i + 1))
                for k in range(TOPK):
                    if k == 0:
                        dve.wait_ge(a_first, n + 1)
                    else:
                        dve.wait_ge(d_sum, n * TOPK + k)
                    dve.scalar_tensor_tensor(out=y[:, t, :], in0=got[:, r, k, :],
                                                   scalar=weight_all[:, ds(n), k:k + 1].rearrange("p a k -> p (a k)"),
                                                   in1=y[:, t, :], op0=ALU.mult, op1=ALU.add).then_inc(d_sum, 1)

            def finish(c, t):
                n, r = c * TPC + t, t % 2
                i = c * (TPC // 2) + t // 2
                dve.wait_ge(d_sum, n * TOPK + TOPK)
                dve.bn_stats(stats[:, :], y[:, t, :]).then_inc(d_stat, 1)
                dve.wait_ge(d_stat, 3 * n + 1)
                dve.wait_ge(d_z, n)
                dve.nop(nofuse=True)
                dve.bn_aggr(mv[:, :], stats[:, :]).then_inc(d_stat, 1)
                dve.wait_ge(d_stat, 3 * n + 2)
                dve.tensor_scalar(mv[:, 1:2], mv[:, 1:2], LN_EPS, None, ALU.add).then_inc(d_stat, 1)
                dve.wait_ge(p_rstd, n + 1)
                dve.wait_ge(st_out[r], 16 * i)
                dve.tensor_scalar(z[:, r, :], y[:, t, :], mv[:, 0:1], rstd[:, 0:1], ALU.subtract,
                                  ALU.mult).then_inc(d_z, 1)
                dve.wait_ge(d_z, n + 1)
                dve.wait_ge(in_x1[r], 16 * (i + 1))
                dve.tensor_tensor(z[:, r, :], z[:, r, :], x_mid[:, r, :], ALU.add).then_inc(d_out, 1)

            def indices(c):
                dve.wait_ge(in_rows[0], 16 * TOPK * c * (TPC // 2))
                dve.wait_ge(in_rows[1], 16 * TOPK * c * (TPC // 2))
                dve.tensor_copy(slot[:, :, :], slot_all[:, ds(c * TPC, TPC), :]).then_inc(d_slot, 1)

            def slot_work(c, f):
                hid_low(c, f)
                if f % 2 == 0:
                    turned(c + 1, f // 2)
                if tile_due(c, f):
                    (add_rows, finish)[f % 2](*tile_due(c, f))
                if f == 6:
                    indices(c)

            def after():
                add_rows(NCH - 2, TPC - 1)
                finish(NCH - 2, TPC - 1)
                for t in range(TPC):
                    add_rows(NCH - 1, t)
                    finish(NCH - 1, t)
            walk(dve, before, slot_work, after)

        @block.tensor
        def _(pe):
            pe.wait_ge(in_const, 16)

            def turn(c, t):
                n = c * TPC + t
                pe.wait_ge(in_x2, 16 * n + 16)
                pe.wait_ge(d_xt, n)
                for b in range(KC):
                    last = pe.transpose(turn_ps[:, b * P:(b + 1) * P], x_in[:, t % 2, b * P:(b + 1) * P], ident[:, :])
                last.then_inc(t_xt, 1)

            def before():
                for t in range(TPC):
                    turn(0, t)

            def up(c, f):
                k = c * FB + f
                if known(c) and c == 0 and f == 0:
                    pe.wait_ge(d_set, 1)
                pe.wait_ge(d_xt, (c + 1) * TPC)
                pe.wait_ge(a_relu, due(k - 1))
                for b in range(KC):
                    at = ds(f * P, P)
                    last = three(pe, up_ps[f % 2][:, :], (up_h[:, b, at], up_l[:, b, at]),
                                 (xt_h[:, ds(c % 2), b, :].rearrange("p a s -> p (a s)"),
                                  xt_l[:, ds(c % 2), b, :].rearrange("p a s -> p (a s)")),
                                 first=b == 0, last=b == KC - 1)
                last.then_inc(t_up, 1)

            def down(c, f):
                k = c * FB + f
                if known(c) and c == 0 and f == 0:
                    pe.wait_ge(d_set, 2)
                pe.wait_ge(d_hid, k + 1)
                for t in range(TPC):
                    if f == 0:
                        pe.wait_ge(a_first, due((c - 1) * TPC + t + 1))
                    at = ds(t * P, P)
                    last = three(pe, down_ps[t][:, :], (hid_h[:, f % 2, at], hid_l[:, f % 2, at]),
                                 (down_h[:, f, :], down_l[:, f, :]), first=f == 0, last=f == FB - 1)
                    last.then_inc(t_down, 1)

            def slot(c, f):
                up(c, f)
                if f % 2 == 0:
                    turn(c + 1, f // 2)
                if not known(c) or c > 0 or f >= 2:
                    down(*back2(c, f))

            def after():
                down(NCH - 1, FB - 2)
                down(NCH - 1, FB - 1)
            walk(pe, before, slot, after)


def layer(nc, d, out):
    def scratch(name, shape):
        return nc.dram_tensor(name, shape, F32).ap()

    x1, x2 = (scratch(n, [NT, P, C]) for n in ("x_mid_rows", "x_norm_rows"))
    slots, rows = scratch("slot_rows", [NSLOT, C]), scratch("expert_rows", [NSLOT, C])
    with nc.sbuf_tensor("slot_all", [P, NT, TOPK], U32) as slot_all, \
         nc.sbuf_tensor("weight_all", [P, NT, TOPK], F32) as weight_all:
        phase_attention(nc, d, x1, x2, slots, (slot_all, weight_all))
        phase_experts(nc, d, slots, rows)
        phase_shared(nc, d, x1, x2, rows, (slot_all, weight_all), out)


def kernel(L0_attn_hidden_states, L0_attn_Wq, L0_attn_bq, L0_attn_Wk, L0_attn_bk, L0_attn_Wv, L0_attn_bv,
           L0_attn_Wo, L0_ffn_gate_w, L0_ffn_bias_corr, L0_ffn_up_w, L0_ffn_down_w, L0_ffn_shared_up_w,
           L0_ffn_shared_down_w):
    import concourse.bacc as bacc
    import numpy as np
    from concourse.bass_utils import run_bass_kernel_spmd

    def turned(w, blocks):
        w = np.asarray(w)
        return w.reshape(w.shape[0], blocks, P).transpose(2, 1, 0)

    def each_turned(w, blocks):
        w = np.asarray(w)
        n, o, i = w.shape
        return w.reshape(n, o, blocks, P).transpose(0, 3, 2, 1).reshape(n, P, blocks * o)

    def repeated(row, *shape):
        return np.broadcast_to(row, (P, *shape))

    arrays = {
        "x": np.asarray(L0_attn_hidden_states).reshape(NT, P, C),
        "wq": each_turned(np.asarray(L0_attn_Wq).reshape(H, D, C), KC),
        "wk": turned(L0_attn_Wk, KC),
        "wv": turned(L0_attn_Wv, KC),
        "wo": np.asarray(L0_attn_Wo).reshape(C, H, D).transpose(1, 2, 0),
        "bq": np.asarray(L0_attn_bq).reshape(H, D).T,
        "bk": np.asarray(L0_attn_bk).reshape(1, HD2),
        "bv": np.asarray(L0_attn_bv).reshape(1, HD2),
        "gate": turned(L0_ffn_gate_w, KC),
        "bias_corr": repeated(np.asarray(L0_ffn_bias_corr), TPC, NE),
        "up": each_turned(L0_ffn_up_w, KC),
        "down": each_turned(L0_ffn_down_w, FE // P),
        "shared_up": turned(L0_ffn_shared_up_w, KC).reshape(P, KC * FS),
        "shared_down": turned(L0_ffn_shared_down_w, FS // P).reshape(P, FS // P * C),
        "ident": np.eye(P, dtype=np.float32),
        "ones": np.ones((P, P), np.float32),
        "before_me": np.triu(np.ones((P, P), np.float32), 1),
        "keep": repeated(np.array([0] + [1] * (TPB - 1), np.float32), TPB),
        "iota": repeated(np.arange(NE, dtype=np.float32), TPC * TOPK, NE),
        "iota_g": repeated(np.tile(np.arange(NG, dtype=np.float32), TPC)[:, None], TPC * NG, TOPG),
    }
    arrays = {f"in_{k}": np.ascontiguousarray(v) for k, v in arrays.items()}
    nc = bacc.Bacc("TRN2", target_bir_lowering=False, num_devices=1)
    d = {k[3:]: nc.dram_tensor(k, v.shape, mybir.dt.from_np(v.dtype), kind="ExternalInput").ap()
         for k, v in arrays.items()}
    out = nc.dram_tensor("out", [NT, P, C], F32, kind="ExternalOutput").ap()
    layer(nc, d, out)
    got = run_bass_kernel_spmd(nc, [arrays], core_ids=[0])
    return got.results[0]["out"].reshape(B, S, C)
```

```python
from contextlib import ExitStack

import concourse.bass as bass
from concourse import mybir

F32 = mybir.dt.float32
F32R = mybir.dt.float32r
U32 = mybir.dt.uint32
ALU = mybir.AluOpType
ACT = mybir.ActivationFunctionType
AX = mybir.AxisListType

P = 128
B, S, C = 4, 1024, 512
T = B * S
NT = T // P
KC = C // P
CH = 512
NCH = T // CH
TPC = CH // P
TPB = S // P
H, G, D = 16, 4, 128
HPG = H // G
HD2 = G * D
NE, NG, TOPG, TOPK = 32, 8, 4, 4
EPG = NE // NG
CAP = 256
NSLOT = NE * CAP
FE, FS = 256, 1024
LN_EPS, NORM_EPS, SCALE = 1e-5, 1e-6, 2.5
SKIP = float(1 << 20)

assert G == TPC and NT == NCH * G


def ds(i, k=1):
    return bass.ds(i, k)


def known(v):
    return isinstance(v, int)


def back(n, j, lag):
    return (n, j - lag) if j >= lag else (n - 1, j - lag + HPG)


def due(value):
    return max(value, 0) if known(value) else value


def three(pe, out, lhs, rhs, first=True, last=True):
    pe.matmul(out, lhs[0], rhs[0], start=first, stop=False, skip_group_check=True)
    pe.matmul(out, lhs[0], rhs[1], start=False, stop=False, skip_group_check=True)
    return pe.matmul(out, lhs[1], rhs[0], start=False, stop=last, skip_group_check=True)


def flat(ap):
    n = len(ap.shape)
    if n == 3:
        return ap.rearrange("p a n -> p (a n)")
    return ap.rearrange("p a c n -> p (a c) n")


SCATTERS = {(1, 2): (0, 3), (1, 3): (3, 7), (2, 0): (7, 10), (2, 1): (10, 13), (2, 2): (13, 16)}
ROUTE = 49


def phase_attention(nc, d, x1, x2, slots, kept):
    slot_all, weight_all = kept
    with ExitStack() as ctx:
        def sb(name, shape, dt=F32):
            return ctx.enter_context(nc.sbuf_tensor("a_" + name, shape, dt))

        def sem(name):
            return ctx.enter_context(nc.semaphore("a_" + name))

        ident = sb("ident", [P, P])
        ones, ones_r = sb("ones", [P, P]), sb("ones_r", [P, P], F32R)
        keep = sb("keep", [P, TPB])
        power = sb("power", [P, TPC])
        wk_h, wk_l = sb("wk_h", [P, KC, HD2], F32R), sb("wk_l", [P, KC, HD2], F32R)
        wv_h, wv_l = sb("wv_h", [P, KC, HD2], F32R), sb("wv_l", [P, KC, HD2], F32R)
        bq = sb("bq", [P, H])
        bkv = sb("bkv", [2, 2, HD2], F32R)
        xT_h, xT_l = sb("xT_h", [P, 3, KC, CH], F32R), sb("xT_l", [P, 3, KC, CH], F32R)
        kv, ksum = sb("kv", [P, 2, HD2]), sb("ksum", [P, 2, G])
        x_in, xn = sb("x_in", [P, C]), sb("xn", [P, C])
        stats, mv, rstd = sb("stats", [P, 6]), sb("mv", [P, 2]), sb("rstd", [P, 1])
        xt_h, xt_l = sb("xt_h", [P, KC, P], F32R), sb("xt_l", [P, KC, P], F32R)
        k_exp, sk = sb("k_exp", [P, HD2]), sb("sk", [P, HD2])
        sk_h, sk_l = sb("sk_h", [P, HD2], F32R), sb("sk_l", [P, HD2], F32R)
        sk_sum = sb("sk_sum", [P, HD2])
        v_h, v_l = sb("v_h", [P, HD2], F32R), sb("v_l", [P, HD2], F32R)
        wq_raw, wo_raw = sb("wq_raw", [P, 2, KC, P]), sb("wo_raw", [P, 2, C])
        wq_h, wq_l = sb("wq_h", [P, 2, KC, P], F32R), sb("wq_l", [P, 2, KC, P], F32R)
        wo_h, wo_l = sb("wo_h", [P, 2, C], F32R), sb("wo_l", [P, 2, C], F32R)
        q_both = sb("q_both", [P, 2, CH])
        q_exp, q_pos = q_both[:, 0, :], q_both[:, 1, :]
        sq, sqn = sb("sq", [P, 2, CH]), sb("sqn", [P, CH])
        sqn_h, sqn_l = sb("sqn_h", [P, CH], F32R), sb("sqn_l", [P, CH], F32R)
        rn = sb("rn", [P, TPC])
        kv_h, kv_l = sb("kv_h", [P, D], F32R), sb("kv_l", [P, D], F32R)
        o_h, o_l = sb("o_h", [P, 2, CH], F32R), sb("o_l", [P, 2, CH], F32R)
        acc = sb("acc", [P, 2, TPC, C])
        x_res, x_norm = sb("x_res", [P, 2, C]), sb("x_norm", [P, TPC, C])
        zeros = x_res[:, 0, :]
        xt_norm = sb("xt_norm", [P, TPC, KC, P])
        stats1, mv1, rstd1 = sb("stats1", [P, TPC, 6]), sb("mv1", [P, TPC, 2]), sb("rstd1", [P, TPC])
        stats2, mv2, rstd2 = sb("stats2", [P, TPC, 6]), sb("mv2", [P, TPC, 2]), sb("rstd2", [P, TPC])
        before_me, bias = sb("before_me", [P, P]), sb("bias", [P, TPC, NE])
        iota = sb("iota", [P, TPC * TOPK, NE])
        iota_g = sb("iota_g", [P, TPC * NG, TOPG])
        gate = sb("gate", [P, KC, NE])
        ex, score, corr, masked = (sb(n, [P, TPC, NE]) for n in ("ex", "score", "corr", "masked"))
        hi2, lo2 = sb("hi2", [P, TPC * NG, 2]), sb("lo2", [P, TPC * NG, 2])
        top, second, third, gsum, gmask = (sb(n, [P, TPC * NG]) for n in ("top", "second", "third", "gsum", "gmask"))
        g8, gi, g_hot = sb("g8", [P, TPC, 8]), sb("gi", [P, TPC, 8], U32), sb("g_hot", [P, TPC, NG, TOPG])
        e8, ei = sb("e8", [P, TPC, 8]), sb("ei", [P, TPC, 8], U32)
        hot = sb("hot", [P, TPC, TOPK, NE])
        hot_part = xt_norm[:, 0, :, :].rearrange("p t (k e) -> p t k e", k=TOPK)
        chosen, earlier = sb("chosen", [P, TPC, NE]), sb("earlier", [P, TPC, NE])
        weight, place, over, slot_f, fits = (sb(n, [P, TPC, TOPK]) for n in ("weight", "place", "over", "slot_f", "fits"))
        wsum, winv = sb("wsum", [P, TPC]), sb("winv", [P, TPC])
        slot_of = sb("slot_of", [P, TPC, TOPK], U32)
        bkv_raw, bkv_low, bkv_high = sq[0:2, :, :], q_both[0:2, :, :], o_h[0:2, :, :]

        def bank(name):
            return ctx.enter_context(nc.psum_tensor("a_" + name, [P, CH], F32))

        out_ps = [bank(f"out_ps{t}") for t in range(TPC)]
        q_ps, n_ps, o_ps, m_ps = bank("q_ps"), bank("n_ps"), bank("o_ps"), bank("m_ps")
        BESIDE, ALONE = (m_ps, m_ps, m_ps, m_ps), (n_ps, q_ps, o_ps, out_ps[3])

        def blocks(ps):
            return ps[:, :].rearrange("p (c s) -> p c s", c=KC)
        by_expert = m_ps[:, 0:TPC * NE].rearrange("p (t e) -> p t e", t=TPC)

        in_const, in_x, in_ident, in_wv, in_route = (sem(n) for n in ("in_const", "in_x", "in_ident", "in_wv", "in_route"))
        in_wq, in_wo, in_res = ([sem(f"in_{n}{r}") for r in range(2)] for n in ("wq", "wo", "res"))
        st_zero = sem("st_zero")
        acc_free = sem("acc_free")
        a_set, p_set, d_set = sem("a_set"), sem("p_set"), sem("d_set")
        d_stat, d_xn = sem("d_stat"), sem("d_xn")
        p_rstd = sem("p_rstd")
        t_xt, a_xt, d_xt, a_xT = sem("t_xt"), sem("a_xt"), sem("d_xt"), sem("a_xT")
        t_k, a_k, d_sk, a_skh, p_skl = sem("t_k"), sem("a_k"), sem("d_sk"), sem("a_skh"), sem("p_skl")
        t_v, a_vh, d_vl = sem("t_v"), sem("a_vh"), sem("d_vl")
        d_sksum = sem("d_sksum")
        t_ks, d_ks, t_kv, d_kv = sem("t_ks"), sem("d_ks"), sem("t_kv"), sem("d_kv")
        a_wq, p_wq, a_wo, p_wo = sem("a_wq"), sem("p_wq"), sem("a_wo"), sem("p_wo")
        t_q, a_q, d_sq = sem("t_q"), sem("a_q"), sem("d_sq")
        t_n, d_rn, t_b = sem("t_n"), sem("d_rn"), sem("t_b")
        d_sqn, a_sqh, p_sql = sem("d_sqn"), sem("a_sqh"), sem("p_sql")
        d_kvg = sem("d_kvg")
        t_o, a_oh, d_ol = sem("t_o"), sem("a_oh"), sem("d_ol")
        t_w, d_acc = sem("t_w"), sem("d_acc")

        st_norm, st_slots = sem("st_norm"), sem("st_slots")
        d_stat1, d_stat2 = sem("d_stat1"), sem("d_stat2")
        p_rstd1, p_rstd2 = sem("p_rstd1"), sem("p_rstd2")
        d_y, d_mid, d_norm = sem("d_y"), sem("d_mid"), sem("d_norm")
        t_xn, a_xn = sem("t_xn"), sem("a_xn")
        t_logit, a_ex, t_place, d_route = sem("t_logit"), sem("a_ex"), sem("t_place"), sem("d_route")
        STAT = 2 * TPC + 1
        CHOSEN, PRIOR, PLACED, SLOTS = 31, 34, 37, 41
        CONST, ROUTE_CONST = 16 * 7, 16 * 5

        block = ctx.enter_context(nc.Block())

        def walk(eng, prep, attn):
            prep(0, True)
            with eng.Fori(1, TPB - 1) as m:
                prep(m, True)
            prep(TPB - 1, False)

            def chunk(c, tiles):
                for g in range(G):
                    attn(c * G + g, c, g, c * G + g + TPB if tiles else None)
            for c in range(3):
                chunk(c, True)
            with eng.Fori(3, NCH - 2) as c:
                chunk(c, True)
            with eng.Fori(NCH - 2, NCH) as c:
                chunk(c, False)
            chunk(NCH, False)
            chunk(NCH + 1, False)

        def live(k):
            return not known(k) or 0 <= k < NT * HPG

        def chunk_due(c, lag):
            return c - lag if not known(c) or 0 <= c - lag < NCH else None

        def is_last(e):
            return known(e) and e == NCH - 1

        def norm_rows(e):
            return acc[:, 0, :, :] if is_last(e) else x_norm[:, :, :]

        def turned_at(c, g):
            return (slice(None), ds(c % 3), slice(None), slice(g * P, (g + 1) * P))

        @block.sync
        def _(sp):
            def load_x(m):
                sp.dma_start(x_in[:, :], d["x"][ds(m), :, :].rearrange("a p c -> (a p) c")).then_inc(in_x, 16)

            def load_wq(k):
                sp.dma_start(wq_raw[:, k % 2, :, :].rearrange("p c d -> p (c d)"),
                             d["wq"][k % H, :, :]).then_inc(in_wq[k % 2], 16)

            def load_wo(k):
                sp.dma_start(wo_raw[:, k % 2, :], d["wo"][k % H, :, :]).then_inc(in_wo[k % 2], 16)

            load_x(0)
            sp.dma_start(ident[:, :], d["ident"]).then_inc(in_ident, 16)
            sp.dma_start(acc[:, 0, :, :], d["wk"]).then_inc(acc_free, 16)
            sp.dma_start(ones[:, :], d["ones"]).then_inc(in_const, 16)
            sp.dma_start(keep[:, :], d["keep"]).then_inc(in_const, 16)
            sp.dma_start(bq[:, :], d["bq"]).then_inc(in_const, 16)
            for w, name in enumerate(("bk", "bv")):
                for row in range(2):
                    sp.dma_start(bkv_raw[row:row + 1, w, :], d[name]).then_inc(in_const, 16)
            sp.dma_start(acc[:, 1, :, :], d["wv"]).then_inc(in_wv, 16)
            load_wq(0)
            load_wq(1)
            for dst, name in ((before_me[:, :], "before_me"), (bias[:, :, :], "bias_corr"), (iota[:, :, :], "iota"),
                              (iota_g[:, :, :], "iota_g"), (gate[:, :, :], "gate")):
                sp.dma_start(dst, d[name]).then_inc(in_route, 16)
            sp.wait_ge(p_set, 2)

            def prep(m, ahead):
                sp.wait_ge(d_xn, m + 1)
                load_x(m + 1)

            def load_res(e, t):
                sp.wait_ge(d_mid, due(TPC * e + t - 1))
                sp.dma_start(x_res[:, t % 2, :], d["x"][ds(e * TPC + t), :, :].rearrange(
                    "a p c -> (a p) c")).then_inc(in_res[t % 2], 16)

            def rows(store, e):
                return store[ds(e * TPC, TPC), :, :].rearrange("t p c -> p t c")

            def beside(c, g, j):
                e = chunk_due(c, 2)
                if e is not None and (g, j) == (0, 0):
                    sp.wait_ge(a_xn, TPC * (e + 1))
                    sp.nop(nofuse=True)
                    sp.wait_ge(st_norm, 16 * e)
                    sp.nop(nofuse=True)
                    sp.dma_start(rows(x2, e), xt_norm[:, :, :, :].rearrange("p t b s -> p t (b s)")).then_inc(st_norm, 16)
                e = chunk_due(c, 1)
                if e is None:
                    return
                if (g, j) == (1, 0):
                    if known(e) and e == 0:
                        sp.wait_ge(st_zero, 16 * 2 * G)
                    load_res(e, 0)
                    load_res(e, 1)
                if (g, j) == (2, 1):
                    load_res(e, 2)
                    load_res(e, 3)
                if (g, j) == (2, 3):
                    sp.wait_ge(d_mid, TPC * (e + 1))
                    sp.dma_start(rows(x1, e), acc[:, ds(e % 2), :, :].rearrange(
                        "p a t c -> p (a t) c")).then_inc(acc_free, 16)

            def attn(n, c, g, m):
                for j in range(HPG):
                    k = n * HPG + j
                    if live(k):
                        if m is not None and j == 1:
                            sp.wait_ge(d_xn, m + 1)
                            load_x((m + 1) % NT)
                        sp.wait_ge(p_wq, k + 1)
                        load_wq(g * HPG + j + 2)
                        sp.wait_ge(p_wo, due(k - 1))
                        load_wo(g * HPG + j)
                    beside(c, g, j)
                if known(n) and n < G:
                    part = NSLOT // (2 * G)
                    for z in (2 * n, 2 * n + 1):
                        sp.dma_start(slots[z * part:(z + 1) * part, :].rearrange("(p r) c -> p r c", p=P),
                                     zeros.rearrange("p (a c) -> p a c", a=1).to_broadcast(
                                         [P, part // P, C])).then_inc(st_zero, 16)

            walk(sp, prep, attn)
            sp.wait_ge(acc_free, 16 * (NCH + 1))
            sp.wait_ge(st_norm, 16 * NCH)
            sp.wait_ge(st_zero, 16 * 2 * G)
            sp.wait_ge(in_x, 16 * (NT + 1))
            for r in range(2):
                sp.wait_ge(in_wq[r], 16 * (NT * HPG // 2 + 1))

        @block.gpsimd
        def _(pool):
            pool.memset(power[:, :], -0.5).then_inc(p_set, 1)
            pool.memset(zeros, 0.0).then_inc(p_set, 1)
            pool.wait_ge(p_set, 2)

            def reciprocal_deviation(m):
                pool.wait_ge(d_stat, 3 * m + 3)
                pool.wait_ge(d_xn, m)
                pool.tensor_tensor(rstd[:, :], mv[:, 1:2], power[:, 0:1], ALU.pow).then_inc(p_rstd, 1)

            def keys_low(m):
                pool.wait_ge(a_skh, m + 1)
                pool.wait_ge(t_kv, m)
                pool.tensor_tensor(sk_l[:, :], sk[:, :], sk_h[:, :].bitcast(F32), ALU.subtract).then_inc(p_skl, 1)

            def wq_low(n, j):
                k = n * HPG + j
                pool.wait_ge(a_wq, k + 1)
                pool.wait_ge(t_q, due(k - 1))
                pool.tensor_tensor(wq_l[:, j % 2, :, :], wq_raw[:, j % 2, :, :],
                                   wq_h[:, j % 2, :, :].bitcast(F32), ALU.subtract).then_inc(p_wq, 1)

            def wo_low(n, j):
                k = n * HPG + j
                pool.wait_ge(a_wo, k + 1)
                pool.wait_ge(t_w, due(4 * (k - 1)))
                pool.tensor_tensor(wo_l[:, j % 2, :], wo_raw[:, j % 2, :], wo_h[:, j % 2, :].bitcast(F32),
                                   ALU.subtract).then_inc(p_wo, 1)

            def sqn_low(n, j):
                k = n * HPG + j
                pool.wait_ge(a_sqh, k + 1)
                pool.wait_ge(t_o, k)
                pool.tensor_tensor(sqn_l[:, :], sqn[:, :], sqn_h[:, :].bitcast(F32),
                                   ALU.subtract).then_inc(p_sql, 1)

            def scatter(e, first, last):
                pool.wait_ge(d_route, ROUTE * e + SLOTS)
                pool.nop(nofuse=True)
                for i in range(first, last):
                    t, k = i // TOPK, i % TOPK
                    pool.indirect_dma_start(slots, bass.IndirectOffsetOnAxis(ap=slot_of[:, t, k:k + 1], axis=0),
                                            norm_rows(e)[:, t, :], None, bounds_check=NSLOT - 1,
                                            oob_is_err=False).then_inc(st_slots, 16)

            def beside(c, g, j):
                e = chunk_due(c, 1)
                if e is not None and (g, j) == (1, 3):
                    pool.wait_ge(d_stat1, STAT * (e + 1))
                    pool.wait_ge(d_y, TPC * e)
                    pool.tensor_tensor(rstd1[:, :], mv1[:, :, 1], power[:, :], ALU.pow).then_inc(p_rstd1, 1)
                if e is not None and (g, j) == (2, 3):
                    pool.wait_ge(d_stat2, STAT * (e + 1))
                    pool.wait_ge(d_norm, TPC * e)
                    pool.tensor_tensor(rstd2[:, :], mv2[:, :, 1], power[:, :], ALU.pow).then_inc(p_rstd2, 1)
                e = chunk_due(c, 2)
                if known(c) and c == NCH:
                    if (g, j) == (2, 3):
                        scatter(e, 0, TPC * TOPK)
                elif e is not None and (g, j) in SCATTERS:
                    if known(e) and e == 0 and (g, j) == (1, 2):
                        pool.wait_ge(st_zero, 16 * 2 * G)
                    scatter(e, *SCATTERS[g, j])

            def prep(m, ahead):
                if known(m) and m == 0:
                    reciprocal_deviation(0)
                if ahead:
                    reciprocal_deviation(m + 1)
                keys_low(m)
                if known(m) and m == 0:
                    wq_low(0, 0)

            def slot(n, j, c, g, m):
                k = n * HPG + j
                if live(k - 2):
                    sqn_low(*back(n, j, 2))
                if live(k + 1):
                    wq_low(*((n, j + 1) if j < HPG - 1 else (n + 1, 0)))
                if m is not None and j == 0:
                    reciprocal_deviation(m)
                if live(k - 2):
                    wo_low(*back(n, j, 2))
                if m is not None and j == 2:
                    keys_low(m)
                beside(c, g, j)

            def attn(n, c, g, m):
                for j in range(HPG):
                    slot(n, j, c, g, m)

            walk(pool, prep, attn)
            pool.wait_ge(st_slots, 16 * TOPK * NT)

        @block.scalar
        def _(act):
            def turned(m, ps=BESIDE):
                act.wait_ge(t_xt, m + 1)
                act.wait_ge(t_v, m)
                act.wait_ge(a_xT, 2 * m)
                act.activation(xt_h[:, :, :], blocks(ps[0]), ACT.Copy).then_inc(a_xt, 1)

            def keep_turned(c, g, m):
                act.wait_ge(a_xt, m + 1)
                act.activation(flat(xT_h[turned_at(c, g)]), xt_h[:, :, :], ACT.Copy).then_inc(a_xT, 1)
                act.wait_ge(d_xt, m + 1)
                act.activation(flat(xT_l[turned_at(c, g)]), xt_l[:, :, :], ACT.Copy).then_inc(a_xT, 1)

            def keys(m, ps=BESIDE):
                act.wait_ge(t_k, m + 1)
                act.wait_ge(p_skl, m)
                if ps is BESIDE:
                    act.wait_ge(d_sksum, m - TPB)
                act.activation(k_exp[:, :], ps[1][:, :], ACT.Exp).then_inc(a_k, 1)
                act.activation(sk[:, :], ps[1][:, :], ACT.Relu).then_inc(a_k, 1)

            def keys_high(m):
                act.wait_ge(d_sk, m + 1)
                act.wait_ge(t_kv, m)
                act.activation(sk_h[:, :], sk[:, :], ACT.Copy).then_inc(a_skh, 1)

            def values(m, ps=BESIDE):
                act.wait_ge(t_v, m + 1)
                act.wait_ge(t_kv, m)
                act.activation(v_h[:, :], ps[2][:, :], ACT.Copy).then_inc(a_vh, 1)

            def wq_high(n, j):
                k = n * HPG + j
                act.wait_ge(in_wq[j % 2], 16 * (2 * n + j // 2 + 1))
                act.wait_ge(t_q, due(k - 1))
                act.wait_ge(p_wq, due(k - 1))
                act.activation(wq_h[:, j % 2, :, :], wq_raw[:, j % 2, :, :], ACT.Copy).then_inc(a_wq, 1)

            def wo_high(n, j):
                k = n * HPG + j
                act.wait_ge(in_wo[j % 2], 16 * (2 * n + j // 2 + 1))
                act.wait_ge(t_w, due(4 * (k - 1)))
                act.activation(wo_h[:, j % 2, :], wo_raw[:, j % 2, :], ACT.Copy).then_inc(a_wo, 1)

            def queries(n, j, g):
                k = n * HPG + j
                act.wait_ge(t_q, k + 1)
                act.wait_ge(d_sq, k)
                bias = bq[:, ds(g * HPG + j)]
                act.activation(q_exp, q_ps[:, :], ACT.Exp, bias=bias).then_inc(a_q, 1)
                act.activation(q_pos, q_ps[:, :], ACT.Relu, bias=bias).then_inc(a_q, 1)

            def sqn_high(n, j):
                k = n * HPG + j
                act.wait_ge(d_sqn, k + 1)
                act.wait_ge(t_o, k)
                act.activation(sqn_h[:, :], sqn[:, :], ACT.Copy).then_inc(a_sqh, 1)

            def o_high(n, j):
                k = n * HPG + j
                act.wait_ge(t_o, k + 1)
                act.wait_ge(t_w, due(4 * (k - 1)))
                act.activation(o_h[:, j % 2, :], o_ps[:, :], ACT.Copy).then_inc(a_oh, 1)

            def turned_alone(m):
                turned(m, ALONE)
                at = (slice(None), ds(m // TPC), slice(None), ds((m % TPC) * P, P))
                act.wait_ge(a_xt, m + 1)
                act.activation(flat(xT_h[at]), xt_h[:, :, :], ACT.Copy).then_inc(a_xT, 1)
                act.wait_ge(d_xt, m + 1)
                act.activation(flat(xT_l[at]), xt_l[:, :, :], ACT.Copy).then_inc(a_xT, 1)

            def prep(m, ahead):
                if known(m) and m == 0:
                    act.wait_ge(acc_free, 16)
                    act.activation(wk_h[:, :, :], acc[:, 0, :, :], ACT.Copy).then_inc(a_set, 1)
                    act.wait_ge(in_const, CONST)
                    turned_alone(0)
                    act.wait_ge(in_wv, 16)
                    act.activation(wv_h[:, :, :], acc[:, 1, :, :], ACT.Copy).then_inc(a_set, 1)
                keys(m, ALONE)
                keys_high(m)
                values(m, ALONE)
                if ahead:
                    turned_alone(m + 1)
                if known(m) and m == 0:
                    wq_high(0, 0)

            def beside_norm(c):
                e = chunk_due(c, 1)
                if e is None:
                    return
                act.wait_ge(t_logit, e)
                act.wait_ge(d_route, due(ROUTE * (e - 1) + 43))
                for t in range(TPC):
                    act.wait_ge(t_xn, TPC * e + t + 1)
                    act.activation(xt_norm[:, t, :, :], out_ps[t][:, :].rearrange("p (c s) -> p c s", c=KC),
                                   ACT.Copy).then_inc(a_xn, 1)

            def beside_logits(c):
                e = chunk_due(c, 2)
                if e is None:
                    return
                act.wait_ge(t_logit, e + 1)
                act.wait_ge(d_route, due(ROUTE * (e - 1) + 2))
                act.activation(ex[:, :, :], by_expert, ACT.Exp, scale=-1.0).then_inc(a_ex, 1)

            def slot(n, j, c, g, m):
                k = n * HPG + j
                if live(k - 2):
                    sqn_high(*back(n, j, 2))
                if m is not None and j == 2:
                    keys(m)
                if m is not None and j == 3:
                    values(m)
                if (g, j) == (3, 3):
                    beside_norm(c)
                if live(k + 1):
                    wq_high(*((n, j + 1) if j < HPG - 1 else (n + 1, 0)))
                if live(k - 2):
                    wo_high(*back(n, j, 2))
                if live(k):
                    queries(n, j, g)
                if (g, j) == (0, 0):
                    beside_logits(c)
                if m is not None and j == 1:
                    turned(m)
                    keep_turned(c + 2, g, m)
                if m is not None and j == 2:
                    keys_high(m)
                if live(k - 2):
                    o_high(*back(n, j, 2))

            def attn(n, c, g, m):
                for j in range(HPG):
                    slot(n, j, c, g, m)

            walk(act, prep, attn)

        @block.vector
        def _(dve):
            def normed(m):
                dve.wait_ge(in_x, 16 * m + 16)
                dve.bn_stats(stats[:, :], x_in[:, :]).then_inc(d_stat, 1)
                dve.wait_ge(d_stat, 3 * m + 1)
                dve.wait_ge(d_xn, m)
                dve.nop(nofuse=True)
                dve.bn_aggr(mv[:, :], stats[:, :]).then_inc(d_stat, 1)
                dve.wait_ge(d_stat, 3 * m + 2)
                dve.tensor_scalar(mv[:, 1:2], mv[:, 1:2], LN_EPS, None, ALU.add).then_inc(d_stat, 1)

            def scaled(m):
                dve.wait_ge(p_rstd, m + 1)
                dve.wait_ge(t_xt, m)
                dve.tensor_scalar(xn[:, :], x_in[:, :], mv[:, 0:1], rstd[:, 0:1], ALU.subtract,
                                  ALU.mult).then_inc(d_xn, 1)

            def turned_low(m, ps=BESIDE):
                dve.wait_ge(a_xt, m + 1)
                dve.wait_ge(t_v, m)
                dve.wait_ge(a_xT, 2 * m)
                dve.tensor_tensor(xt_l[:, :, :], blocks(ps[0]), xt_h[:, :, :].bitcast(F32),
                                  ALU.subtract).then_inc(d_xt, 1)

            def keys(m):
                dve.wait_ge(a_k, 2 * m + 2)
                dve.scalar_tensor_tensor(out=sk[:, :], in0=k_exp[:, :], scalar=1.0, in1=sk[:, :],
                                         op0=ALU.min, op1=ALU.add).then_inc(d_sk, 1)

            def values_low(m, ps=BESIDE):
                dve.wait_ge(a_vh, m + 1)
                dve.wait_ge(t_kv, m)
                dve.tensor_tensor(v_l[:, :], ps[2][:, :], v_h[:, :].bitcast(F32), ALU.subtract).then_inc(d_vl, 1)

            def sum_keys(m, g):
                if g == 0:
                    dve.wait_ge(t_ks, m // TPC + TPB - 2)
                    dve.wait_ge(d_sk, m + 1)
                    dve.tensor_copy(sk_sum[:, :], sk[:, :]).then_inc(d_sksum, 1)
                else:
                    dve.wait_ge(d_sksum, m - TPB)
                    dve.tensor_tensor(sk_sum[:, :], sk_sum[:, :], sk[:, :], ALU.add).then_inc(d_sksum, 1)

            def chunk_key_sums(m):
                q = m // TPC
                at = flat(ksum[:, ds((q // 2) % 2), :])
                dve.wait_ge(t_ks, q + TPB - 1)
                dve.wait_ge(d_ks, q + TPB - 2)
                dve.scalar_tensor_tensor(out=at, in0=at, scalar=keep[:, ds(q % 2)], in1=m_ps[:, 0:2 * G:2],
                                         op0=ALU.mult, op1=ALU.add).then_inc(d_ks, 1)

            def key_sums(m, ps):
                at = flat(ksum[:, ds((m // TPB) % 2), :])
                dve.wait_ge(t_ks, m + 1)
                dve.wait_ge(d_ks, m)
                dve.scalar_tensor_tensor(out=at, in0=at, scalar=keep[:, ds(m % TPB)], in1=ps[3][:, 0:2 * G:2],
                                         op0=ALU.mult, op1=ALU.add).then_inc(d_ks, 1)

            def state(m):
                at = flat(kv[:, ds((m // TPB) % 2), :])
                dve.wait_ge(t_kv, m + 1)
                dve.wait_ge(d_kv, m)
                dve.scalar_tensor_tensor(out=at, in0=at, scalar=keep[:, ds(m % TPB)], in1=m_ps[:, :],
                                         op0=ALU.mult, op1=ALU.add).then_inc(d_kv, 1)

            def queries(n, j):
                k = n * HPG + j
                dve.wait_ge(a_q, 2 * k + 2)
                dve.wait_ge(t_n, due(k - 1))
                dve.wait_ge(d_sqn, due(k - 1))
                dve.scalar_tensor_tensor(out=sq[:, j % 2, :], in0=q_exp, scalar=1.0, in1=q_pos,
                                         op0=ALU.min, op1=ALU.add).then_inc(d_sq, 1)

            def norms(n, j):
                k = n * HPG + j
                dve.wait_ge(t_n, k + 1)
                dve.wait_ge(t_b, k)
                dve.tensor_scalar(rn[:, :], n_ps[:, 0:TPC], NORM_EPS, None, ALU.add).then_inc(d_rn, 1)
                dve.wait_ge(d_rn, 2 * k + 1)
                dve.reciprocal(rn[:, :], rn[:, :]).then_inc(d_rn, 1)

            def normal(n, j):
                k = n * HPG + j
                dve.wait_ge(t_b, k + 1)
                dve.wait_ge(p_sql, k)
                dve.tensor_tensor(sqn[:, :], n_ps[:, :], sq[:, j % 2, :], ALU.mult).then_inc(d_sqn, 1)

            def o_low(n, j):
                k = n * HPG + j
                dve.wait_ge(a_oh, k + 1)
                dve.wait_ge(t_w, due(4 * (k - 1)))
                dve.tensor_tensor(o_l[:, j % 2, :], o_ps[:, :], o_h[:, j % 2, :].bitcast(F32),
                                  ALU.subtract).then_inc(d_ol, 1)

            def group_state(n, g):
                src = flat(kv[:, ds((n // TPB) % 2), ds(g * D, D)])
                dve.wait_ge(t_o, HPG * n)
                dve.wait_ge(d_kv, (n // TPB + 1) * TPB)
                dve.tensor_copy(kv_h[:, :], src).then_inc(d_kvg, 1)
                dve.wait_ge(d_kvg, 2 * n + 1)
                dve.tensor_tensor(kv_l[:, :], src, kv_h[:, :].bitcast(F32), ALU.subtract).then_inc(d_kvg, 1)

            def accumulate(n, c):
                dve.wait_ge(acc_free, 16 * c)
                dve.wait_ge(d_norm, due(TPC * (c - 1)))
                for t in range(TPC):
                    at = flat(acc[:, ds(c % 2), t, :])
                    dve.wait_ge(t_w, 4 * (HPG * n + HPG - 1) + t + 1)
                    dve.wait_ge(d_acc, 4 * n)
                    dve.scalar_tensor_tensor(out=at, in0=at, scalar=keep[:, ds(n % G)], in1=out_ps[t][:, :],
                                             op0=ALU.mult, op1=ALU.add).then_inc(d_acc, 1)

            def prep(m, ahead):
                if known(m) and m == 0:
                    dve.memset(kv[:, :, :], 0.0).then_inc(d_set, 1)
                    dve.memset(ksum[:, :, :], 0.0).then_inc(d_set, 1)
                    dve.memset(earlier[:, :, :], 0.0).then_inc(d_set, 1)
                    normed(0)
                    scaled(0)
                    dve.wait_ge(in_const, CONST)
                    dve.tensor_copy(ones_r[:, :], ones[:, :]).then_inc(d_set, 1)
                    dve.tensor_copy(bkv_high, bkv_raw).then_inc(d_set, 1)
                    dve.wait_ge(d_set, 5)
                    dve.tensor_tensor(bkv_low, bkv_raw, bkv_high.bitcast(F32),
                                      ALU.subtract).then_inc(d_set, 1)
                    dve.wait_ge(d_set, 6)
                    dve.tensor_scalar(bkv_raw, bkv_high.bitcast(F32), ident[0:2, 0:1],
                                      None, ALU.mult).then_inc(d_set, 1)
                    dve.wait_ge(d_set, 7)
                    for w in range(2):
                        dve.scalar_tensor_tensor(out=bkv[:, w, :], in0=bkv_low[:, w, :], scalar=ident[0:2, 1:2],
                                                 in1=bkv_raw[:, w, :], op0=ALU.mult, op1=ALU.add).then_inc(d_set, 1)
                    dve.wait_ge(a_set, 1)
                    dve.tensor_tensor(wk_l[:, :, :], acc[:, 0, :, :], wk_h[:, :, :].bitcast(F32),
                                      ALU.subtract).then_inc(d_set, 1)
                    turned_low(0, ALONE)
                    dve.wait_ge(a_set, 2)
                    dve.tensor_tensor(wv_l[:, :, :], acc[:, 1, :, :], wv_h[:, :, :].bitcast(F32),
                                      ALU.subtract).then_inc(d_set, 1)
                    dve.wait_ge(d_set, 11)
                if ahead:
                    normed(m + 1)
                    scaled(m + 1)
                keys(m)
                values_low(m, ALONE)
                if ahead:
                    turned_low(m + 1, ALONE)
                key_sums(m, ALONE)
                state(m)

            def tile(e, t):
                return flat(acc[:, ds(e % 2), t, :])

            def statistics(e, tiles, st, steps, mv_read):
                for t in tiles:
                    if t == 0:
                        dve.wait_ge(mv_read, TPC * e)
                    if steps is d_stat1:
                        dve.wait_ge(d_acc, TPC * G * e + TPC * (G - 1) + t + 1)
                        dve.nop(nofuse=True)
                    else:
                        dve.wait_ge(d_mid, TPC * e + t + 1)
                        dve.nop(nofuse=True)
                    dve.bn_stats(st[:, t, :], tile(e, t)).then_inc(steps, 1)

            def aggregate(e, st, v, steps):
                dve.wait_ge(steps, STAT * e + TPC)
                dve.nop(nofuse=True)
                for t in range(TPC):
                    dve.bn_aggr(v[:, t, :], st[:, t, :]).then_inc(steps, 1)
                dve.wait_ge(steps, STAT * e + 2 * TPC)
                dve.tensor_scalar(v[:, :, 1], v[:, :, 1], LN_EPS, None, ALU.add).then_inc(steps, 1)

            def normal_output(e):
                dve.wait_ge(p_rstd1, e + 1)
                for t in range(TPC):
                    dve.tensor_scalar(tile(e, t), tile(e, t), mv1[:, t, 0:1], rstd1[:, t:t + 1],
                                      ALU.subtract, ALU.mult).then_inc(d_y, 1)

            def residual(e, tiles):
                for t in tiles:
                    dve.wait_ge(in_res[t % 2], 16 * (2 * e + t // 2 + 1))
                    dve.wait_ge(d_y, TPC * e + t + 1)
                    dve.tensor_tensor(tile(e, t), tile(e, t), x_res[:, t % 2, :], ALU.add).then_inc(d_mid, 1)

            def normal_residual(e):
                dve.wait_ge(p_rstd2, e + 1)
                if is_last(e):
                    dve.wait_ge(acc_free, 16 * NCH)
                    dve.wait_ge(d_norm, TPC * e)
                else:
                    dve.wait_ge(st_slots, 16 * TOPK * TPC * e)
                dve.wait_ge(t_xn, TPC * e)
                for t in range(TPC):
                    dve.tensor_scalar(norm_rows(e)[:, t, :], tile(e, t), mv2[:, t, 0:1], rstd2[:, t:t + 1],
                                      ALU.subtract, ALU.mult).then_inc(d_norm, 1)

            def quads(ap):
                return ap[:, :, :].rearrange("p t (g a b) -> p (t g) a b", a=2, b=2)

            def done(e, n):
                dve.wait_ge(d_route, ROUTE * e + n)

            def choose(e, part):
                if part == 0:
                    if known(e) and e == 0:
                        dve.wait_ge(in_route, ROUTE_CONST)
                    dve.wait_ge(a_ex, e + 1)
                    dve.tensor_scalar(ex[:, :, :], ex[:, :, :], 1.0, None, ALU.add).then_inc(d_route, 1)
                    done(e, 1)
                    dve.reciprocal(score[:, :, :], ex[:, :, :]).then_inc(d_route, 1)
                    done(e, 2)
                    dve.tensor_tensor(corr[:, :, :], score[:, :, :], bias[:, :, :], ALU.add).then_inc(d_route, 1)
                    done(e, 3)
                    groups = quads(corr)
                    dve.tensor_tensor(hi2[:, :, :], groups[:, :, :, 0], groups[:, :, :, 1], ALU.max).then_inc(d_route, 1)
                    dve.tensor_tensor(lo2[:, :, :], groups[:, :, :, 0], groups[:, :, :, 1], ALU.min).then_inc(d_route, 1)
                    done(e, 5)
                    dve.tensor_tensor(top[:, :], hi2[:, :, 0], hi2[:, :, 1], ALU.max).then_inc(d_route, 1)
                    dve.tensor_tensor(second[:, :], hi2[:, :, 0], hi2[:, :, 1], ALU.min).then_inc(d_route, 1)
                    dve.tensor_tensor(third[:, :], lo2[:, :, 0], lo2[:, :, 1], ALU.max).then_inc(d_route, 1)
                    done(e, 8)
                    dve.tensor_tensor(gsum[:, :], second[:, :], third[:, :], ALU.max).then_inc(d_route, 1)
                    done(e, 9)
                    dve.tensor_tensor(gsum[:, :], top[:, :], gsum[:, :], ALU.add).then_inc(d_route, 1)
                if part == 1:
                    dve.wait_ge(d_route, ROUTE * e + 10)
                    dve.nop(nofuse=True)
                    for t in range(TPC):
                        dve.max(g8[:, t, :], gsum[:, t * NG:(t + 1) * NG]).then_inc(d_route, 1)
                    dve.wait_ge(d_route, ROUTE * e + 14)
                    dve.nop(nofuse=True)
                    for t in range(TPC):
                        dve.max_index(gi[:, t, :], g8[:, t, :], gsum[:, t * NG:(t + 1) * NG]).then_inc(d_route, 1)
                    done(e, 18)
                    dve.tensor_tensor(g_hot[:, :, :, :], iota_g[:, :, :].rearrange("p (t g) k -> p t g k", t=TPC),
                                      gi[:, :, 0:TOPG].rearrange("p t (a k) -> p t a k", a=1).to_broadcast(
                                          [P, TPC, NG, TOPG]), ALU.is_equal).then_inc(d_route, 1)
                    done(e, 19)
                    dve.tensor_reduce(gmask[:, :], g_hot[:, :, :, :].rearrange("p t g k -> p (t g) k"), AX.X,
                                      ALU.add).then_inc(d_route, 1)
                    done(e, 20)
                    dve.tensor_tensor(masked[:, :, :].rearrange("p t (g e) -> p (t g) e", g=NG),
                                      corr[:, :, :].rearrange("p t (g e) -> p (t g) e", g=NG),
                                      gmask[:, :].rearrange("p (g a) -> p g a", a=1).to_broadcast([P, TPC * NG, EPG]),
                                      ALU.mult).then_inc(d_route, 1)
                if part == 2:
                    dve.wait_ge(d_route, ROUTE * e + 21)
                    dve.nop(nofuse=True)
                    for t in range(TPC):
                        dve.max(e8[:, t, :], masked[:, t, :]).then_inc(d_route, 1)
                    dve.wait_ge(d_route, ROUTE * e + 25)
                    dve.nop(nofuse=True)
                    for t in range(TPC):
                        dve.max_index(ei[:, t, :], e8[:, t, :], masked[:, t, :]).then_inc(d_route, 1)
                    done(e, 29)
                    dve.tensor_tensor(hot[:, :, :, :], iota[:, :, :].rearrange("p (t k) e -> p t k e", t=TPC),
                                      ei[:, :, 0:TOPK].rearrange("p t (k a) -> p t k a", a=1).to_broadcast(
                                          [P, TPC, TOPK, NE]), ALU.is_equal).then_inc(d_route, 1)
                    done(e, 30)
                    dve.tensor_reduce(chosen[:, :, :], hot[:, :, :, :].rearrange("p t k e -> p t e k"), AX.X,
                                      ALU.add).then_inc(d_route, 1)
                    for t in range(1, TPC):
                        done(e, CHOSEN + t - 1)
                        dve.tensor_tensor(earlier[:, t, :], earlier[:, t - 1, :], chosen[:, t - 1, :],
                                          ALU.add).then_inc(d_route, 1)

            def count_earlier(e):
                dve.wait_ge(st_norm, 16 * (e + 1))
                dve.wait_ge(t_place, e + 1)
                dve.tensor_tensor(hot_part, hot[:, :, :, :],
                                  by_expert.rearrange("p t (a e) -> p t a e", a=1).to_broadcast(
                                      [P, TPC, TOPK, NE]), ALU.mult).then_inc(d_route, 1)
                done(e, 35)
                dve.tensor_reduce(place[:, :, :], hot_part, AX.X, ALU.add).then_inc(d_route, 1)
                dve.tensor_tensor(earlier[:, 0, :], earlier[:, TPC - 1, :], chosen[:, TPC - 1, :],
                                  ALU.add).then_inc(d_route, 1)

            def slots_and_weights(e):
                done(e, PLACED)
                dve.tensor_scalar(over[:, :, :], place[:, :, :], float(CAP), SKIP, ALU.is_ge,
                                  ALU.mult).then_inc(d_route, 1)
                dve.scalar_tensor_tensor(out=slot_f[:, :, :], in0=ei[:, :, 0:TOPK], scalar=float(CAP),
                                         in1=place[:, :, :], op0=ALU.mult, op1=ALU.add).then_inc(d_route, 1)
                dve.tensor_scalar(fits[:, :, :], place[:, :, :], float(CAP), None, ALU.is_lt).then_inc(d_route, 1)
                done(e, 40)
                dve.wait_ge(st_slots, 16 * TOPK * TPC * e)
                dve.tensor_tensor(slot_of[:, :, :], slot_f[:, :, :], over[:, :, :], ALU.add).then_inc(d_route, 1)
                dve.tensor_tensor(hot_part, hot[:, :, :, :],
                                  score[:, :, :].rearrange("p t (a e) -> p t a e", a=1).to_broadcast(
                                      [P, TPC, TOPK, NE]), ALU.mult).then_inc(d_route, 1)
                done(e, 42)
                dve.tensor_reduce(weight[:, :, :], hot_part, AX.X, ALU.add).then_inc(d_route, 1)
                done(e, 43)
                dve.tensor_reduce(wsum[:, :], weight[:, :, :], AX.X, ALU.add).then_inc(d_route, 1)
                done(e, 44)
                dve.tensor_scalar(wsum[:, :], wsum[:, :], 1e-20, None, ALU.add).then_inc(d_route, 1)
                done(e, 45)
                dve.reciprocal(winv[:, :], wsum[:, :]).then_inc(d_route, 1)
                done(e, 46)
                dve.scalar_tensor_tensor(out=weight[:, :, :], in0=weight[:, :, :], scalar=SCALE,
                                         in1=winv[:, :].rearrange("p (t a) -> p t a", a=1).to_broadcast([P, TPC, TOPK]),
                                         op0=ALU.mult, op1=ALU.mult).then_inc(d_route, 1)
                done(e, 47)
                dve.tensor_tensor(weight_all[:, ds(e * TPC, TPC), :], weight[:, :, :], fits[:, :, :],
                                  ALU.mult).then_inc(d_route, 1)
                dve.tensor_copy(slot_all[:, ds(e * TPC, TPC), :], slot_of[:, :, :]).then_inc(d_route, 1)

            def beside(c, g, j):
                e = chunk_due(c, 1)
                if e is not None:
                    if (g, j) == (1, 0):
                        statistics(e, (0, 1), stats1, d_stat1, d_y)
                    if (g, j) == (1, 3):
                        statistics(e, (2, 3), stats1, d_stat1, d_y)
                        aggregate(e, stats1, mv1, d_stat1)
                    if (g, j) == (2, 0):
                        normal_output(e)
                    if (g, j) == (2, 1):
                        residual(e, (0, 1))
                        statistics(e, (0, 1), stats2, d_stat2, d_norm)
                    if (g, j) == (2, 2):
                        residual(e, (2, 3))
                    if (g, j) == (2, 3):
                        statistics(e, (2, 3), stats2, d_stat2, d_norm)
                        aggregate(e, stats2, mv2, d_stat2)
                    if (g, j) == (3, 0):
                        normal_residual(e)
                e = chunk_due(c, 2)
                if e is not None:
                    if g == 0 and j >= 1:
                        choose(e, j - 1)
                    if (g, j) == (1, 0):
                        count_earlier(e)
                    if (g, j) == (1, 1):
                        slots_and_weights(e)

            def slot(n, j, c, g, m):
                k = n * HPG + j
                if live(k - 2):
                    normal(*back(n, j, 2))
                if j == 3 and live(k - 4):
                    accumulate(n - 1, c if g else c - 1)
                if m is not None and j == 0:
                    normed(m)
                if m is not None and j == 3:
                    values_low(m)
                    sum_keys(m, g)
                if live(k - 1):
                    norms(*back(n, j, 1))
                if m is not None and j == 1:
                    turned_low(m)
                if live(k):
                    queries(n, j)
                if m is not None and j == 0:
                    scaled(m)
                if m is not None and j == 2:
                    keys(m)
                if m is not None and j == 3 and g == TPC - 1:
                    chunk_key_sums(m)
                beside(c, g, j)
                if m is not None and j == 3:
                    state(m)
                if live(k - 2):
                    o_low(*back(n, j, 2))
                if j == 1 and live(k):
                    group_state(n, g)

            def attn(n, c, g, m):
                for j in range(HPG):
                    slot(n, j, c, g, m)

            walk(dve, prep, attn)

        @block.tensor
        def _(pe):
            def turn(m, ps=BESIDE):
                pe.wait_ge(d_xn, m + 1)
                if ps is BESIDE:
                    pe.wait_ge(d_kv, m)
                else:
                    pe.wait_ge(d_xt, m)
                for b in range(KC):
                    last = pe.transpose(blocks(ps[0])[:, b, :], xn[:, b * P:(b + 1) * P], ident[:, :])
                last.then_inc(t_xt, 1)

            def project(out, w_h, w_l, bias):
                pe.matmul(out[:, :], ones_r[0:2, :], bkv[:, bias, :], start=True, stop=False,
                          skip_group_check=True)
                for b in range(KC):
                    last = three(pe, out[:, :], (xt_h[:, b, :], xt_l[:, b, :]), (w_h[:, b, :], w_l[:, b, :]),
                                 first=False, last=b == KC - 1)
                return last

            def keys(m, ps=BESIDE):
                pe.wait_ge(d_xt, m + 1)
                pe.wait_ge(a_k, 2 * m)
                project(ps[1], wk_h, wk_l, 0).then_inc(t_k, 1)

            def values(m, ps=BESIDE):
                if ps is BESIDE:
                    pe.wait_ge(a_k, 2 * m + 2)
                else:
                    pe.wait_ge(d_vl, m)
                project(ps[2], wv_h, wv_l, 1).then_inc(t_v, 1)

            def chunk_key_sums(m):
                pe.wait_ge(d_sksum, m + 1 - TPB)
                pe.wait_ge(d_vl, m + 1)
                for g in range(G):
                    last = pe.matmul(m_ps[:, 2 * g:2 * g + 1], sk_sum[:, ds(g * D, D)], ones[:, 0:1], start=True,
                                     stop=True, skip_group_check=True)
                last.then_inc(t_ks, 1)

            def key_sums(m, ps):
                pe.wait_ge(p_skl, m + 1)
                pe.wait_ge(d_ks, m)
                for g in range(G):
                    at = ds(g * D, D)
                    pe.matmul(ps[3][:, 2 * g:2 * g + 2], sk_h[:, at], ones_r[:, 0:2], start=True, stop=False,
                              skip_group_check=True)
                    last = pe.matmul(ps[3][:, 2 * g:2 * g + 2], sk_l[:, at], ones_r[:, 0:2], start=False,
                                     stop=True, skip_group_check=True)
                last.then_inc(t_ks, 1)

            def key_values(m, g=None):
                pe.wait_ge(p_skl, m + 1)
                pe.wait_ge(d_vl, m + 1)
                if g is None:
                    pe.wait_ge(d_kv, m)
                elif g == TPC - 1:
                    pe.wait_ge(d_ks, m // TPC + TPB - 1)
                for g in range(G):
                    at = ds(g * D, D)
                    last = three(pe, m_ps[:, at], (sk_h[:, at], sk_l[:, at]), (v_h[:, at], v_l[:, at]))
                last.then_inc(t_kv, 1)

            def query(n, j, c):
                k = n * HPG + j
                r, at = j % 2, ds(c % 3)
                pe.wait_ge(p_wq, k + 1)
                pe.wait_ge(a_q, 2 * k)
                if j == 0:
                    pe.wait_ge(a_xT, 2 * (c + 1) * TPC)
                for b in range(KC):
                    last = three(pe, q_ps[:, :], (wq_h[:, r, b, :], wq_l[:, r, b, :]),
                                 (xT_h[:, at, b, :].rearrange("p a s -> p (a s)"),
                                  xT_l[:, at, b, :].rearrange("p a s -> p (a s)")),
                                 first=b == 0, last=b == KC - 1)
                last.then_inc(t_q, 1)

            def norm(n, j):
                k = n * HPG + j
                sums = ksum[:, ds((n // TPB) % 2), ds(n % G)].rearrange("p a s -> p (a s)")
                pe.wait_ge(d_sq, k + 1)
                pe.wait_ge(d_sqn, k)
                pe.wait_ge(d_ks, TPB + 2 * (n // TPB))
                for t in range(TPC):
                    last = pe.matmul(n_ps[:, t:t + 1], sq[:, j % 2, t * P:(t + 1) * P], sums, start=True,
                                     stop=True, skip_group_check=True)
                last.then_inc(t_n, 1)

            def spread(n, j):
                k = n * HPG + j
                pe.wait_ge(d_rn, 2 * k + 2)
                for t in range(TPC):
                    last = pe.transpose(n_ps[:, t * P:(t + 1) * P], rn[:, t:t + 1].to_broadcast([P, P]),
                                        ident[:, :])
                last.then_inc(t_b, 1)

            def attend(n, j):
                k = n * HPG + j
                pe.wait_ge(p_sql, k + 1)
                pe.wait_ge(d_kvg, 2 * n + 2)
                pe.wait_ge(d_ol, k)
                three(pe, o_ps[:, :], (kv_h[:, :], kv_l[:, :]), (sqn_h[:, :], sqn_l[:, :])).then_inc(t_o, 1)

            def output(n, j, turned_chunk):
                k = n * HPG + j
                pe.wait_ge(d_ol, k + 1)
                pe.wait_ge(p_wo, k + 1)
                for t in range(TPC):
                    if j == 0:
                        pe.wait_ge(d_acc, due(4 * (n - 1) + t + 1))
                    if j == 0 and turned_chunk is not None:
                        pe.wait_ge(a_xn, TPC * turned_chunk + t + 1)
                    at = ds(t * P, P)
                    three(pe, out_ps[t][:, :], (o_h[:, j % 2, at], o_l[:, j % 2, at]),
                          (wo_h[:, j % 2, :], wo_l[:, j % 2, :]), first=j == 0,
                          last=j == HPG - 1).then_inc(t_w, 1)

            def prep(m, ahead):
                if known(m) and m == 0:
                    pe.wait_ge(in_ident, 16)
                    turn(0, ALONE)
                    pe.wait_ge(in_const, CONST)
                    pe.wait_ge(d_set, 10)
                keys(m, ALONE)
                if ahead:
                    turn(m + 1, ALONE)
                if known(m) and m == 0:
                    pe.wait_ge(d_set, 11)
                values(m, ALONE)
                key_sums(m, ALONE)
                key_values(m)

            def steps_done(n):
                return min(n, NT) if known(n) else n

            def turn_norm(e, n):
                for t in range(TPC):
                    pe.wait_ge(d_norm, TPC * e + t + 1)
                    pe.wait_ge(d_acc, TPC * steps_done(n))
                    for b in range(KC):
                        last = pe.transpose(out_ps[t][:, b * P:(b + 1) * P], norm_rows(e)[:, t, b * P:(b + 1) * P],
                                            ident[:, :])
                    last.then_inc(t_xn, 1)

            def logits(e, m):
                if known(e) and e == 0:
                    pe.wait_ge(in_route, ROUTE_CONST)
                pe.wait_ge(a_xn, TPC * (e + 1))
                pe.wait_ge(d_kv, NT if m is None else m)
                for t in range(TPC):
                    for b in range(KC):
                        last = pe.matmul(by_expert[:, t, :], xt_norm[:, t, b, :], gate[:, b, :], start=b == 0,
                                         stop=b == KC - 1, skip_group_check=True)
                last.then_inc(t_logit, 1)

            def places(e, m):
                pe.wait_ge(d_route, ROUTE * e + PRIOR)
                pe.wait_ge(d_kv, NT if m is None else m)
                pe.matmul(by_expert, before_me[:, :], chosen[:, :, :], start=True, stop=False,
                          skip_group_check=True)
                pe.matmul(by_expert, ones[:, :], earlier[:, :, :], start=False, stop=True,
                          skip_group_check=True).then_inc(t_place, 1)

            def slot(n, j, c, g, m):
                k = n * HPG + j
                e1, e2 = chunk_due(c, 1), chunk_due(c, 2)
                if live(k):
                    query(n, j, c)
                if live(k - 1):
                    norm(*back(n, j, 1))
                if e1 is not None and (g, j) == (3, 3):
                    turn_norm(e1, n)
                if e2 is not None and (g, j) == (1, 0):
                    places(e2, m)
                if m is not None and j == 1:
                    if e2 is not None and g == 0:
                        pe.wait_ge(a_ex, e2 + 1)
                    if e2 is not None and g == 1:
                        pe.wait_ge(d_route, ROUTE * e2 + CHOSEN + 4)
                    turn(m)
                if m is not None and j == 3 and g == TPC - 1:
                    chunk_key_sums(m)
                if live(k - 3):
                    output(*back(n, j, 3), e1 if g == 3 else None)
                if e2 is not None and (g, j) == (0, 0):
                    logits(e2, m)
                if m is not None and j == 3:
                    key_values(m, g)
                if live(k - 2):
                    attend(*back(n, j, 2))
                if live(k - 1):
                    spread(*back(n, j, 1))
                if m is not None and j == 1:
                    keys(m)
                if m is not None and j == 2:
                    values(m)

            def attn(n, c, g, m):
                for j in range(HPG):
                    slot(n, j, c, g, m)

            walk(pe, prep, attn)


def phase_experts(nc, d, slots, rows):
    FB = FE // P
    SB = CAP // P
    with ExitStack() as ctx:
        def sb(name, shape, dt=F32):
            return ctx.enter_context(nc.sbuf_tensor("e_" + name, shape, dt))

        def sem(name):
            return ctx.enter_context(nc.semaphore("e_" + name))

        def bank(name):
            return ctx.enter_context(nc.psum_tensor("e_" + name, [P, 512], F32))

        ident = sb("ident", [P, P])
        x_in = sb("x_in", [P, 2, SB, C])
        up, up_h, up_l = sb("up", [P, 2, KC * FE]), sb("up_h", [P, 2, KC * FE], F32R), sb("up_l", [P, 2, KC * FE], F32R)
        down, down_h, down_l = sb("down", [P, 2, FB * C]), sb("down_h", [P, 2, FB * C], F32R), sb("down_l", [P, 2, FB * C], F32R)
        xt_h, xt_l = sb("xt_h", [P, 2, KC, CAP], F32R), sb("xt_l", [P, 2, KC, CAP], F32R)
        relu, hid = sb("relu", [P, FB * CAP]), sb("hid", [P, FB * CAP])
        hid_h, hid_l = sb("hid_h", [P, 2, FB, CAP], F32R), sb("hid_l", [P, 2, FB, CAP], F32R)
        y = sb("y", [P, 2, SB, C])
        turn_ps = [bank(f"turn_ps{i}") for i in range(2)]
        up_ps = [bank(f"up_ps{i}") for i in range(2)]
        down_ps = [bank(f"down_ps{i}") for i in range(4)]

        in_const = sem("in_const")
        in_x, in_up, in_down = ([sem(f"{n}{i}") for i in range(2)] for n in ("in_x", "in_up", "in_down"))
        t_xt, a_xt, d_xt = sem("t_xt"), sem("a_xt"), sem("d_xt")
        d_up, p_up, a_down, p_down = sem("d_up"), sem("p_up"), sem("a_down"), sem("p_down")
        t_up, a_relu, d_hid, a_hid, d_hidl = sem("t_up"), sem("a_relu"), sem("d_hid"), sem("a_hid"), sem("d_hidl")
        t_down, a_y, d_y = sem("t_down"), sem("a_y"), sem("d_y")
        st_y = [sem(f"st_y{i}") for i in range(2)]
        block = ctx.enter_context(nc.Block())

        def walk(eng, slot, lag):
            for e in range(4):
                slot(e, e % 2, e // 2)
            with eng.Fori(2, NE // 2) as i:
                slot(2 * i, 0, i)
                slot(2 * i + 1, 1, i)
            for e in range(NE, NE + lag):
                slot(e, e % 2, e // 2)

        def live(e, lag=0):
            return not known(e) or 0 <= e - lag < NE

        @block.sync
        def _(sp):
            sp.dma_start(ident[:, :], d["ident"]).then_inc(in_const, 16)

            def slot(e, r, i):
                if live(e):
                    sp.wait_ge(t_xt, due(2 * (e - 1)))
                    sp.dma_start(x_in[:, r, :, :], slots[ds(e * CAP, CAP), :].rearrange(
                        "(s p) c -> p s c", p=P)).then_inc(in_x[r], 16)
                    sp.wait_ge(d_up, due(e - 1))
                    sp.wait_ge(p_up, due(e - 1))
                    sp.dma_start(up[:, r, :], d["up"][ds(e), :, :].rearrange("a p n -> (a p) n")).then_inc(in_up[r], 16)
                    sp.wait_ge(a_down, due(e - 1))
                    sp.wait_ge(p_down, due(e - 1))
                    sp.dma_start(down[:, r, :], d["down"][ds(e), :, :].rearrange("a p n -> (a p) n")).then_inc(in_down[r], 16)
            walk(sp, slot, 0)

        @block.gpsimd
        def _(pool):
            def slot(e, r, i):
                if live(e):
                    pool.wait_ge(d_up, e + 1)
                    pool.wait_ge(t_up, due(e - 1))
                    pool.tensor_tensor(up_l[:, r, :], up[:, r, :], up_h[:, r, :].bitcast(F32),
                                       ALU.subtract).then_inc(p_up, 1)
                    pool.wait_ge(a_down, e + 1)
                    pool.wait_ge(t_down, due(2 * (e - 1)))
                    pool.tensor_tensor(down_l[:, r, :], down[:, r, :], down_h[:, r, :].bitcast(F32),
                                       ALU.subtract).then_inc(p_down, 1)
            walk(pool, slot, 0)

        @block.scalar
        def _(act):
            def slot(e, r, i):
                q = 1 - r
                if live(e):
                    for b in range(2):
                        act.wait_ge(t_xt, 2 * e + b + 1)
                        if b == 0:
                            act.wait_ge(t_up, due(e - 1))
                        act.activation(xt_h[:, r, 2 * b:2 * b + 2, :],
                                       turn_ps[b][:, :].rearrange("p (c s) -> p c s", c=2),
                                       ACT.Copy).then_inc(a_xt, 1)
                if live(e, 1):
                    act.wait_ge(t_up, e)
                    act.wait_ge(d_hid, due(e - 1))
                    act.activation(relu[:, :], up_ps[q][:, :], ACT.Relu).then_inc(a_relu, 1)
                    act.wait_ge(d_hid, e)
                    act.wait_ge(t_down, due(2 * (e - 2)))
                    act.activation(hid_h[:, q, :, :].rearrange("p a b -> p (a b)"), hid[:, :],
                                   ACT.Copy).then_inc(a_hid, 1)
                if live(e):
                    act.wait_ge(in_down[r], 16 * i + 16)
                    act.wait_ge(t_down, due(2 * (e - 1)))
                    act.wait_ge(p_down, due(e - 1))
                    act.activation(down_h[:, r, :], down[:, r, :], ACT.Copy).then_inc(a_down, 1)
                if live(e, 2):
                    act.wait_ge(t_down, due(2 * (e - 2) + 1))
                    act.wait_ge(st_y[r], due(16 * (i - 1)))
                    act.activation(y[:, r, 0, :], down_ps[2 * r][:, :], ACT.Copy).then_inc(a_y, 1)
                if live(e, 3):
                    act.wait_ge(a_y, due(e - 2))
                    act.wait_ge(d_y, due(e - 2))
                    act.dma_start(rows[ds((e - 3) * CAP, CAP), :].rearrange("(s p) c -> p s c", p=P),
                                  y[:, q, :, :]).then_inc(st_y[q], 16)
            walk(act, slot, 3)
            for r in range(2):
                act.wait_ge(st_y[r], 16 * (NE // 2))

        @block.vector
        def _(dve):
            def slot(e, r, i):
                q = 1 - r
                if live(e):
                    dve.wait_ge(in_up[r], 16 * i + 16)
                    dve.wait_ge(t_up, due(e - 1))
                    dve.wait_ge(p_up, due(e - 1))
                    dve.tensor_copy(up_h[:, r, :], up[:, r, :]).then_inc(d_up, 1)
                    for b in range(2):
                        dve.wait_ge(a_xt, 2 * e + b + 1)
                        dve.tensor_tensor(xt_l[:, r, 2 * b:2 * b + 2, :],
                                          turn_ps[b][:, :].rearrange("p (c s) -> p c s", c=2),
                                          xt_h[:, r, 2 * b:2 * b + 2, :].bitcast(F32),
                                          ALU.subtract).then_inc(d_xt, 1)
                if live(e, 1):
                    dve.wait_ge(a_relu, e)
                    dve.wait_ge(a_hid, due(e - 1))
                    dve.wait_ge(d_hidl, due(e - 1))
                    dve.scalar_tensor_tensor(out=hid[:, :], in0=up_ps[q][:, :], scalar=0.0, in1=relu[:, :],
                                             op0=ALU.max, op1=ALU.mult).then_inc(d_hid, 1)
                    dve.wait_ge(a_hid, e)
                    dve.tensor_tensor(hid_l[:, q, :, :].rearrange("p a b -> p (a b)"), hid[:, :],
                                      hid_h[:, q, :, :].rearrange("p a b -> p (a b)").bitcast(F32),
                                      ALU.subtract).then_inc(d_hidl, 1)
                if live(e, 2):
                    dve.wait_ge(t_down, due(2 * (e - 2) + 2))
                    dve.wait_ge(st_y[r], due(16 * (i - 1)))
                    dve.tensor_copy(y[:, r, 1, :], down_ps[2 * r + 1][:, :]).then_inc(d_y, 1)
            walk(dve, slot, 2)

        @block.tensor
        def _(pe):
            pe.wait_ge(in_const, 16)

            def slot(e, r, i):
                q = 1 - r
                if live(e):
                    pe.wait_ge(in_x[r], 16 * i + 16)
                    for b in range(KC):
                        if b % 2 == 0:
                            pe.wait_ge(d_xt, due(2 * (e - 1) + b // 2 + 1))
                        for s in range(SB):
                            last = pe.transpose(turn_ps[b // 2][:, (b % 2) * CAP + s * P:(b % 2) * CAP + (s + 1) * P],
                                                x_in[:, r, s, b * P:(b + 1) * P], ident[:, :])
                        if b % 2 == 1:
                            last.then_inc(t_xt, 1)
                if live(e, 1):
                    pe.wait_ge(d_xt, 2 * e)
                    pe.wait_ge(p_up, e)
                    pe.wait_ge(d_hid, due(e - 2))
                    for f in range(FB):
                        out = up_ps[q][:, f * CAP:(f + 1) * CAP]
                        for b in range(KC):
                            at = ds(b * FE + f * P, P)
                            last = three(pe, out, (up_h[:, q, at], up_l[:, q, at]),
                                         (xt_h[:, q, b, :], xt_l[:, q, b, :]), first=b == 0, last=b == KC - 1)
                    last.then_inc(t_up, 1)
                if live(e, 2):
                    pe.wait_ge(d_hidl, due(e - 1))
                    pe.wait_ge(p_down, due(e - 1))
                    for s in range(SB):
                        pe.wait_ge((a_y, d_y)[s], due(e - 3))
                        for f in range(FB):
                            at, to = ds(s * P, P), ds(f * C, C)
                            last = three(pe, down_ps[2 * r + s][:, :], (hid_h[:, r, f, at], hid_l[:, r, f, at]),
                                         (down_h[:, r, to], down_l[:, r, to]), first=f == 0, last=f == FB - 1)
                        last.then_inc(t_down, 1)
            walk(pe, slot, 2)


def phase_shared(nc, d, x1, x2, rows, kept, out):
    slot_all, weight_all = kept
    FB = FS // P
    with ExitStack() as ctx:
        def sb(name, shape, dt=F32):
            return ctx.enter_context(nc.sbuf_tensor("s_" + name, shape, dt))

        def sem(name):
            return ctx.enter_context(nc.semaphore("s_" + name))

        def bank(name):
            return ctx.enter_context(nc.psum_tensor("s_" + name, [P, 512], F32))

        power = sb("power", [P, 1])
        up, down = sb("up", [P, KC, FS]), sb("down", [P, FB, C])
        up_h, up_l = sb("up_h", [P, KC, FS], F32R), sb("up_l", [P, KC, FS], F32R)
        down_h, down_l = sb("down_h", [P, FB, C], F32R), sb("down_l", [P, FB, C], F32R)
        x_in = sb("x_in", [P, TPC, C])
        xt_h, xt_l = sb("xt_h", [P, 2, KC, CH], F32R), sb("xt_l", [P, 2, KC, CH], F32R)
        relu, hid = sb("relu", [P, CH]), sb("hid", [P, CH])
        hid_h, hid_l = sb("hid_h", [P, 2, CH], F32R), sb("hid_l", [P, 2, CH], F32R)
        got = sb("got", [P, 2, TOPK, C])
        slot = sb("slot", [P, TPC, TOPK], U32)
        y, x_mid, z = sb("y", [P, 2, TPC, C]), sb("x_mid", [P, 2, C]), sb("z", [P, 2, C])
        stats, mv, rstd = sb("stats", [P, 2, 6]), sb("mv", [P, 2, 2]), sb("rstd", [P, 2])
        up_ps = [bank(f"up_ps{i}") for i in range(2)]
        down_ps = [bank(f"down_ps{t}") for t in range(TPC)]

        in_x2 = [sem(f"in_x2{t}") for t in range(TPC)]
        PIECES = FB // 2
        in_up, in_down = ([sem(f"in_{n}{p}") for p in range(PIECES)] for n in ("up", "down"))
        a_up, d_up, a_down, d_down = (sem(n) for n in ("a_up", "d_up", "a_down", "d_down"))
        in_x1 = [sem(f"in_x1{i}") for i in range(2)]
        in_rows, st_out = [sem(f"in_rows{i}") for i in range(2)], [sem(f"st_out{i}") for i in range(2)]
        p_set = sem("p_set")
        a_xt, d_xt = sem("a_xt"), sem("d_xt")
        t_up, a_relu, a_sq, a_hid, d_hid = sem("t_up"), sem("a_relu"), sem("a_sq"), sem("a_hid"), sem("d_hid")
        t_down, d_slot = sem("t_down"), sem("d_slot")
        d_close, d_sum, d_stat, p_rstd, d_z, d_out = (sem(n) for n in ("d_close", "d_sum", "d_stat", "p_rstd", "d_z", "d_out"))
        block = ctx.enter_context(nc.Block())

        def walk(eng, before, slot, after):
            before()
            for c in range(2):
                for f in range(FB):
                    slot(c, f)
            with eng.Fori(2, NCH - 1) as c:
                for f in range(FB):
                    slot(c, f)
            for f in range(FB):
                slot(NCH - 1, f)
            after()

        def finish_due(c, f):
            owner, t = (c - 1, f // 2 - 1) if f >= 2 else (c - 2, TPC - 1)
            return (owner, t) if f % 2 == 0 and (not known(c) or owner >= 0) else None

        def last(c):
            return known(c) and c == NCH - 1

        def piece(w, p):
            return w[:, :, p * 2 * P:(p + 1) * 2 * P] if w.shape[2] == FS else w[:, 2 * p:2 * p + 2, :]

        def back2(c, f):
            return (c, f - 2) if f >= 2 else (c - 1, f - 2 + FB)

        @block.sync
        def _(sp):

            def load_x2(c, t):
                sp.wait_ge(d_xt, due((c - 1) * TPC + t + 1))
                sp.dma_start(x_in[:, t, :], x2[ds((c * TPC + t) % NT), :, :].rearrange(
                    "a p c -> (a p) c")).then_inc(in_x2[t], 16)

            def load_piece(p):
                sp.dma_start(piece(up, p), piece(d["shared_up"], p)).then_inc(in_up[p], 16)
                sp.dma_start(piece(down, p), piece(d["shared_down"], p)).then_inc(in_down[p], 16)

            def before():
                load_x2(0, 0)
                load_piece(0)
                for t in range(1, TPC):
                    load_x2(0, t)
                load_piece(1)
                load_x2(1, 0)
                for p in range(2, PIECES):
                    load_piece(p)

            def residual(c, t):
                n, r = c * TPC + t, t % 2
                sp.wait_ge(d_out, due(n - 1))
                sp.dma_start(x_mid[:, r, :], x1[ds(n), :, :].rearrange("a p c -> (a p) c")).then_inc(in_x1[r], 16)

            def result(c, t):
                n, r = c * TPC + t, t % 2
                sp.wait_ge(d_out, n + 1)
                sp.dma_start(out[ds(n), :, :].rearrange("a p c -> (a p) c"), z[:, r, :]).then_inc(st_out[r], 16)

            def slot(c, f):
                if f % 2 == 0 and not last(c):
                    load_x2(*((c + 1, f // 2 + 1) if f // 2 + 1 < TPC else (c + 2, 0)))
                if f % 2 == 1 and finish_due(c, f - 1):
                    result(*finish_due(c, f - 1))
                ahead = finish_due(c, f + 1) if f < FB - 1 else finish_due(c + 1, 0)
                if ahead:
                    residual(*ahead)

            def after():
                residual(NCH - 1, 0)
                result(NCH - 2, TPC - 1)
                for t in range(TPC):
                    if t + 1 < TPC:
                        residual(NCH - 1, t + 1)
                    result(NCH - 1, t)
                for r in range(2):
                    sp.wait_ge(st_out[r], 16 * NT // 2)
                sp.wait_ge(in_x2[0], 16 * (NCH + 1))
            walk(sp, before, slot, after)

        @block.gpsimd
        def _(pool):
            pool.memset(power[:, :], -0.5).then_inc(p_set, 1)
            pool.memset(got[:, :, :, :], 0.0).then_inc(p_set, 1)
            pool.wait_ge(p_set, 2)

            def gather(c, t):
                n, r = c * TPC + t, t % 2
                pool.wait_ge(d_slot, c + 1)
                pool.wait_ge(d_sum, due(TOPK * (n - 1)))
                pool.nop(nofuse=True)
                for k in range(TOPK):
                    pool.indirect_dma_start(got[:, r, k, :], None, rows,
                                            bass.IndirectOffsetOnAxis(ap=slot[:, t, k:k + 1], axis=0),
                                            bounds_check=NSLOT - 1, oob_is_err=False).then_inc(in_rows[r], 16)

            def deviation(c, t):
                n, r = c * TPC + t, t % 2
                pool.wait_ge(d_stat, 3 * n + 3)
                pool.wait_ge(d_z, due(n - 1))
                pool.tensor_tensor(rstd[:, r:r + 1], mv[:, r, 1:2], power[:, :], ALU.pow).then_inc(p_rstd, 1)

            def slot_work(c, f):
                if finish_due(c, f):
                    deviation(*finish_due(c, f))
                if f in (1, 3, 5):
                    gather(c, f // 2 + 1)
                if f == FB - 1 and not last(c):
                    gather(c + 1, 0)

            def after():
                deviation(NCH - 2, TPC - 1)
                for t in range(TPC):
                    deviation(NCH - 1, t)
            walk(pool, lambda: gather(0, 0), slot_work, after)
            for r in range(2):
                pool.wait_ge(in_rows[r], 16 * TOPK * NT // 2)

        @block.scalar
        def _(act):
            def turned(c, t):
                act.wait_ge(in_x2[t], 16 * (c + 1))
                act.activation(xt_h[:, ds(c % 2), :, ds(t * P, P)].rearrange("p a c s -> p (a c) s"),
                               x_in[:, t, :].rearrange("p (c s) -> p c s", c=KC), ACT.Copy).then_inc(a_xt, 1)

            def up_high(p):
                act.wait_ge(in_up[p], 16)
                act.activation(piece(up_h, p), piece(up, p), ACT.Copy).then_inc(a_up, 1)

            def down_high(p):
                act.wait_ge(in_down[p], 16)
                act.activation(piece(down_h, p), piece(down, p), ACT.Copy).then_inc(a_down, 1)

            def before():
                turned(0, 0)
                up_high(0)
                for t in range(1, TPC):
                    turned(0, t)

            def hidden(c, f):
                k = c * FB + f
                act.wait_ge(t_up, k + 1)
                act.wait_ge(a_sq, k)
                act.activation(relu[:, :], up_ps[f % 2][:, :], ACT.Relu).then_inc(a_relu, 1)
                act.wait_ge(a_relu, k + 1)
                act.wait_ge(a_hid, k)
                act.wait_ge(d_hid, k)
                act.activation(hid[:, :], relu[:, :], ACT.Square).then_inc(a_sq, 1)
                act.wait_ge(a_sq, k + 1)
                act.wait_ge(t_down, due(TPC * (k - 1)))
                act.activation(hid_h[:, f % 2, :], hid[:, :], ACT.Copy).then_inc(a_hid, 1)

            def slot(c, f):
                hidden(c, f)
                if f % 2 == 0 and not last(c):
                    turned(c + 1, f // 2)
                    if known(c) and c == 0:
                        down_high(f // 2)
                        if f // 2 + 1 < PIECES:
                            up_high(f // 2 + 1)
            walk(act, before, slot, lambda: None)

        @block.vector
        def _(dve):
            def turned(c, t):
                n = c * TPC + t
                at = (slice(None), ds(c % 2), slice(None), ds(t * P, P))
                dve.wait_ge(a_xt, n + 1)
                dve.tensor_tensor(xt_l[at].rearrange("p a c s -> p (a c) s"),
                                  x_in[:, t, :].rearrange("p (c s) -> p c s", c=KC),
                                  xt_h[at].rearrange("p a c s -> p (a c) s").bitcast(F32),
                                  ALU.subtract).then_inc(d_xt, 1)

            def up_low(p):
                dve.wait_ge(a_up, p + 1)
                dve.tensor_tensor(piece(up_l, p), piece(up, p), piece(up_h, p).bitcast(F32),
                                  ALU.subtract).then_inc(d_up, 1)

            def down_low(p):
                dve.wait_ge(a_down, p + 1)
                dve.tensor_tensor(piece(down_l, p), piece(down, p), piece(down_h, p).bitcast(F32),
                                  ALU.subtract).then_inc(d_down, 1)

            def before():
                indices(0)
                turned(0, 0)
                up_low(0)
                for t in range(1, TPC):
                    turned(0, t)

            def hid_low(c, f):
                k = c * FB + f
                dve.wait_ge(a_hid, k + 1)
                dve.wait_ge(t_down, due(TPC * (k - 1)))
                dve.tensor_tensor(hid_l[:, f % 2, :], hid[:, :], hid_h[:, f % 2, :].bitcast(F32),
                                  ALU.subtract).then_inc(d_hid, 1)

            def tile(c, t):
                return y[:, ds(c % 2), t, :].rearrange("p a c -> p (a c)")

            def add_rows(c, t):
                n, r = c * TPC + t, t % 2
                i = c * (TPC // 2) + t // 2
                dve.wait_ge(in_rows[r], 16 * TOPK * (i + 1))
                for k in range(TOPK):
                    share = weight_all[:, ds(n), k:k + 1].rearrange("p a k -> p (a k)")
                    if k == 0:
                        dve.wait_ge(d_z, due(TPC * (c - 1)))
                        dve.tensor_scalar(tile(c, t), got[:, r, k, :], share, None, ALU.mult).then_inc(d_sum, 1)
                    else:
                        dve.wait_ge(d_sum, n * TOPK + k)
                        dve.scalar_tensor_tensor(out=tile(c, t), in0=got[:, r, k, :], scalar=share, in1=tile(c, t),
                                                 op0=ALU.mult, op1=ALU.add).then_inc(d_sum, 1)

            def close(c, t):
                dve.wait_ge(d_sum, (c * TPC + t) * TOPK + TOPK)
                dve.wait_ge(t_down, TPC * (c * FB + FB - 1) + t + 1)
                dve.tensor_tensor(tile(c, t), tile(c, t), down_ps[t][:, :], ALU.add).then_inc(d_close, 1)

            def statistics(c, t):
                n, r = c * TPC + t, t % 2
                dve.wait_ge(d_close, n + 1)
                dve.nop(nofuse=True)
                dve.bn_stats(stats[:, r, :], tile(c, t)).then_inc(d_stat, 1)
                dve.wait_ge(d_stat, 3 * n + 1)
                dve.wait_ge(d_z, due(n - 1))
                dve.nop(nofuse=True)
                dve.bn_aggr(mv[:, r, :], stats[:, r, :]).then_inc(d_stat, 1)
                dve.wait_ge(d_stat, 3 * n + 2)
                dve.tensor_scalar(mv[:, r, 1:2], mv[:, r, 1:2], LN_EPS, None, ALU.add).then_inc(d_stat, 1)

            def finish(c, t):
                n, r = c * TPC + t, t % 2
                i = c * (TPC // 2) + t // 2
                dve.wait_ge(p_rstd, n + 1)
                dve.wait_ge(st_out[r], 16 * i)
                dve.tensor_scalar(z[:, r, :], tile(c, t), mv[:, r, 0:1], rstd[:, r:r + 1], ALU.subtract,
                                  ALU.mult).then_inc(d_z, 1)
                dve.wait_ge(d_z, n + 1)
                dve.wait_ge(in_x1[r], 16 * (i + 1))
                dve.tensor_tensor(z[:, r, :], z[:, r, :], x_mid[:, r, :], ALU.add).then_inc(d_out, 1)

            def indices(c):
                dve.wait_ge(in_rows[0], 16 * TOPK * c * (TPC // 2))
                dve.wait_ge(in_rows[1], 16 * TOPK * c * (TPC // 2))
                dve.tensor_copy(slot[:, :, :], slot_all[:, ds(c * TPC, TPC), :]).then_inc(d_slot, 1)

            def slot_work(c, f):
                hid_low(c, f)
                if f % 2 == 0 and not last(c):
                    turned(c + 1, f // 2)
                    if known(c) and c == 0:
                        down_low(f // 2)
                        if f // 2 + 1 < PIECES:
                            up_low(f // 2 + 1)
                if f == 1 and (not known(c) or c > 0):
                    for t in range(TPC):
                        close(c - 1, t)
                if f % 2 == 1:
                    add_rows(c, f // 2)
                if finish_due(c, f):
                    statistics(*finish_due(c, f))
                    finish(*finish_due(c, f))
                if f == FB - 1 and not last(c):
                    indices(c + 1)

            def after():
                statistics(NCH - 2, TPC - 1)
                finish(NCH - 2, TPC - 1)
                for t in range(TPC):
                    close(NCH - 1, t)
                    if t == 1:
                        statistics(NCH - 1, 0)
                for t in range(TPC):
                    if t + 1 < TPC:
                        statistics(NCH - 1, t + 1)
                    finish(NCH - 1, t)
            walk(dve, before, slot_work, after)

        @block.tensor
        def _(pe):
            def up(c, f):
                k = c * FB + f
                if known(c) and c == 0:
                    pe.wait_ge(d_up, f // 2 + 1)
                pe.wait_ge(d_xt, (c + 1) * TPC)
                pe.wait_ge(a_relu, due(k - 1))
                for b in range(KC):
                    at = ds(f * P, P)
                    last = three(pe, up_ps[f % 2][:, :], (up_h[:, b, at], up_l[:, b, at]),
                                 (xt_h[:, ds(c % 2), b, :].rearrange("p a s -> p (a s)"),
                                  xt_l[:, ds(c % 2), b, :].rearrange("p a s -> p (a s)")),
                                 first=b == 0, last=b == KC - 1)
                last.then_inc(t_up, 1)

            def down(c, f):
                k = c * FB + f
                if known(c) and c == 0:
                    pe.wait_ge(d_down, f // 2 + 1)
                pe.wait_ge(d_hid, k + 1)
                for t in range(TPC):
                    if f == 0:
                        pe.wait_ge(d_close, due((c - 1) * TPC + t + 1))
                    at = ds(t * P, P)
                    last = three(pe, down_ps[t][:, :], (hid_h[:, f % 2, at], hid_l[:, f % 2, at]),
                                 (down_h[:, f, :], down_l[:, f, :]), first=f == 0, last=f == FB - 1)
                    last.then_inc(t_down, 1)

            def slot(c, f):
                up(c, f)
                if not known(c) or c > 0 or f >= 2:
                    down(*back2(c, f))

            def after():
                down(NCH - 1, FB - 2)
                down(NCH - 1, FB - 1)
            walk(pe, lambda: None, slot, after)


def layer(nc, d, out):
    def scratch(name, shape):
        return nc.dram_tensor(name, shape, F32).ap()

    x1, x2 = (scratch(n, [NT, P, C]) for n in ("x_mid_rows", "x_norm_turned"))
    slots, rows = scratch("slot_rows", [NSLOT, C]), scratch("expert_rows", [NSLOT, C])
    with nc.sbuf_tensor("slot_all", [P, NT, TOPK], U32) as slot_all, \
         nc.sbuf_tensor("weight_all", [P, NT, TOPK], F32) as weight_all:
        phase_attention(nc, d, x1, x2, slots, (slot_all, weight_all))
        phase_experts(nc, d, slots, rows)
        phase_shared(nc, d, x1, x2, rows, (slot_all, weight_all), out)


def kernel(L0_attn_hidden_states, L0_attn_Wq, L0_attn_bq, L0_attn_Wk, L0_attn_bk, L0_attn_Wv, L0_attn_bv,
           L0_attn_Wo, L0_ffn_gate_w, L0_ffn_bias_corr, L0_ffn_up_w, L0_ffn_down_w, L0_ffn_shared_up_w,
           L0_ffn_shared_down_w):
    import concourse.bacc as bacc
    import numpy as np
    from concourse.bass_utils import run_bass_kernel_spmd

    def turned(w, blocks):
        w = np.asarray(w)
        return w.reshape(w.shape[0], blocks, P).transpose(2, 1, 0)

    def each_turned(w, blocks):
        w = np.asarray(w)
        n, o, i = w.shape
        return w.reshape(n, o, blocks, P).transpose(0, 3, 2, 1).reshape(n, P, blocks * o)

    def repeated(row, *shape):
        return np.broadcast_to(row, (P, *shape))

    arrays = {
        "x": np.asarray(L0_attn_hidden_states).reshape(NT, P, C),
        "wq": each_turned(np.asarray(L0_attn_Wq).reshape(H, D, C), KC),
        "wk": turned(L0_attn_Wk, KC),
        "wv": turned(L0_attn_Wv, KC),
        "wo": np.asarray(L0_attn_Wo).reshape(C, H, D).transpose(1, 2, 0),
        "bq": np.asarray(L0_attn_bq).reshape(H, D).T,
        "bk": np.asarray(L0_attn_bk).reshape(1, HD2),
        "bv": np.asarray(L0_attn_bv).reshape(1, HD2),
        "gate": turned(L0_ffn_gate_w, KC),
        "bias_corr": repeated(np.asarray(L0_ffn_bias_corr), TPC, NE),
        "up": each_turned(L0_ffn_up_w, KC),
        "down": each_turned(L0_ffn_down_w, FE // P),
        "shared_up": turned(L0_ffn_shared_up_w, KC),
        "shared_down": turned(L0_ffn_shared_down_w, FS // P),
        "ident": np.eye(P, dtype=np.float32),
        "ones": np.ones((P, P), np.float32),
        "before_me": np.triu(np.ones((P, P), np.float32), 1),
        "keep": repeated(np.array([0] + [1] * (TPB - 1), np.float32), TPB),
        "iota": repeated(np.arange(NE, dtype=np.float32), TPC * TOPK, NE),
        "iota_g": repeated(np.tile(np.arange(NG, dtype=np.float32), TPC)[:, None], TPC * NG, TOPG),
    }
    arrays = {f"in_{k}": np.ascontiguousarray(v) for k, v in arrays.items()}
    nc = bacc.Bacc("TRN2", target_bir_lowering=False, num_devices=1)
    d = {k[3:]: nc.dram_tensor(k, v.shape, mybir.dt.from_np(v.dtype), kind="ExternalInput").ap()
         for k, v in arrays.items()}
    out = nc.dram_tensor("out", [NT, P, C], F32, kind="ExternalOutput").ap()
    layer(nc, d, out)
    got = run_bass_kernel_spmd(nc, [arrays], core_ids=[0])
    return got.results[0]["out"].reshape(B, S, C)
```
